# Optimizing a Trainium2 kernel written in Bass

```python
import numpy as np
import jax
import jax.numpy as jnp

def _softmax(x, axis=-1):
    return jax.nn.softmax(x, axis=axis)

def _gelu(x):
    return jax.nn.gelu(x, approximate=True)

def _silu(x):
    return jax.nn.silu(x)

def _sigmoid(x):
    return jax.nn.sigmoid(x)

def _layernorm(x, axis=-1, eps=1e-05):
    m = jnp.mean(x, axis=axis, keepdims=True)
    v = jnp.var(x, axis=axis, keepdims=True)
    return (x - m) / jnp.sqrt(v + eps)

def _scatter_add(tgt, idx, src, axis=0):
    return tgt.at[idx].add(src)

def _segment_sum(src, seg, n):
    return jax.ops.segment_sum(src, seg, n)
kernel_name = 'mk_cond_resid_d1_seqx_r2_f433bc'

def setup_inputs(seed: int=0):
    np.random.seed(seed)
    _w = jnp.asarray

    def _rec_inputs():
        import jax
        import jax.numpy as jnp
        _rk = jax.random.key(seed)
        x = 7.22e-05 + 1 * jax.random.normal(jax.random.fold_in(_rk, 1), (16, 512, 512), jnp.float32)
        _lenS = 512 - jax.random.randint(jax.random.fold_in(_rk, 7), (16,), 0, max(1, 512 // 4) + 1, jnp.int32)
        _lenS2 = 512 - jax.random.randint(jax.random.fold_in(_rk, 8), (16,), 0, max(1, 512 // 4) + 1, jnp.int32)
        cond_1024 = 0.00782532 + 1.00527 * jax.random.normal(jax.random.fold_in(_rk, 11), (16, 512), jnp.float32)
        return (x, cond_1024)
    x, cond_1024 = _rec_inputs()

    def _L0_cond_setup():
        import jax, jax.numpy as jnp
        import numpy as np
        EPS = 1e-06
        HEADS = 16

        def _layernorm(x, weight=None):
            mu = jnp.mean(x, axis=-1, keepdims=True)
            var = jnp.var(x, axis=-1, keepdims=True)
            y = (x - mu) / jnp.sqrt(var + EPS)
            return y if weight is None else y * weight

        def _apply_rope(x, position):
            e = x.shape[-1]
            t = x.shape[-2]
            x_rope, x_pass = (x[..., :e // 2], x[..., e // 2:])
            xr = x_rope.reshape(*x_rope.shape[:-1], -1, 2)
            pos = position[:t].reshape(1, 1, t, -1, 2)
            cos, sin = (pos[..., 0], pos[..., 1])
            x0, x1 = (xr[..., 0], xr[..., 1])
            rot = jnp.stack([x0 * cos - x1 * sin, x1 * cos + x0 * sin], axis=-1)
            rot = rot.reshape(*rot.shape[:-2], -1)
            return jnp.concatenate([rot.astype(x.dtype), x_pass], axis=-1)
        key = jax.random.key(seed)
        ks = jax.random.split(key, 8)
        B, T, D, TD = (8, 512, 512, 512)
        e = D // HEADS
        s = 0.02
        return {'x': jax.random.normal(ks[0], (B, T, D), jnp.float32), 'time': jax.random.normal(ks[1], (B, 1, TD), jnp.float32), 'position': jax.random.normal(ks[2], (T, e // 4, 2), jnp.float32), 'mod_w': jax.random.normal(ks[3], (TD, 3 * D), jnp.float32) * s, 'mod_b': jax.random.normal(ks[4], (3 * D,), jnp.float32) * s, 'w_qkv': jax.random.normal(ks[5], (D, 3 * D), jnp.float32) * s, 'w_out': jax.random.normal(ks[6], (D, D), jnp.float32) * s, 'q_norm_w': jnp.ones((e,), jnp.float32), 'k_norm_w': jnp.ones((e,), jnp.float32)}
    _L0_cond_all = _L0_cond_setup()
    _L0_cond_in = {k: v for k, v in _L0_cond_all.items() if k in ('position', 'mod_w', 'mod_b', 'w_qkv', 'w_out', 'q_norm_w', 'k_norm_w')}
    del _L0_cond_all
    return {'x': x, 'cond_1024': cond_1024, 'L0_cond_position': _L0_cond_in['position'], 'L0_cond_mod_w': _L0_cond_in['mod_w'], 'L0_cond_mod_b': _L0_cond_in['mod_b'], 'L0_cond_w_qkv': _L0_cond_in['w_qkv'], 'L0_cond_w_out': _L0_cond_in['w_out'], 'L0_cond_q_norm_w': _L0_cond_in['q_norm_w'], 'L0_cond_k_norm_w': _L0_cond_in['k_norm_w']}

def reference(x, cond_1024, L0_cond_position, L0_cond_mod_w, L0_cond_mod_b, L0_cond_w_qkv, L0_cond_w_out, L0_cond_q_norm_w, L0_cond_k_norm_w):
    import jax
    import jax.numpy as jnp

    def _L0_cond_ref(x, time, position, mod_w, mod_b, w_qkv, w_out, q_norm_w, k_norm_w):
        import jax, jax.numpy as jnp
        import numpy as np
        EPS = 1e-06
        HEADS = 16

        def _layernorm(x, weight=None):
            mu = jnp.mean(x, axis=-1, keepdims=True)
            var = jnp.var(x, axis=-1, keepdims=True)
            y = (x - mu) / jnp.sqrt(var + EPS)
            return y if weight is None else y * weight

        def _apply_rope(x, position):
            e = x.shape[-1]
            t = x.shape[-2]
            x_rope, x_pass = (x[..., :e // 2], x[..., e // 2:])
            xr = x_rope.reshape(*x_rope.shape[:-1], -1, 2)
            pos = position[:t].reshape(1, 1, t, -1, 2)
            cos, sin = (pos[..., 0], pos[..., 1])
            x0, x1 = (xr[..., 0], xr[..., 1])
            rot = jnp.stack([x0 * cos - x1 * sin, x1 * cos + x0 * sin], axis=-1)
            rot = rot.reshape(*rot.shape[:-2], -1)
            return jnp.concatenate([rot.astype(x.dtype), x_pass], axis=-1)
        B, T, D = x.shape
        H = HEADS
        e = D // H
        h = _layernorm(x)
        mod = jax.nn.silu(time) @ mod_w + mod_b
        shift, scale, gate = jnp.split(mod, 3, axis=-1)
        h = h * (scale + 1.0) + shift
        qkv = (h @ w_qkv).reshape(B, T, 3, H, e).transpose(2, 0, 3, 1, 4)
        q, k, v = (qkv[0], qkv[1], qkv[2])
        q = _apply_rope(_layernorm(q, q_norm_w), position)
        k = _apply_rope(_layernorm(k, k_norm_w), position)
        scores = jnp.einsum('bhqe,bhke->bhqk', q, k) / jnp.sqrt(jnp.asarray(e, q.dtype))
        attn = jax.nn.softmax(scores, axis=-1)
        o = jnp.einsum('bhqk,bhke->bhqe', attn, v)
        o = o.transpose(0, 2, 1, 3).reshape(B, T, D)
        return o @ w_out * gate
    x = x + _L0_cond_ref(x, cond_1024[:, None, :], L0_cond_position, L0_cond_mod_w, L0_cond_mod_b, L0_cond_w_qkv, L0_cond_w_out, L0_cond_q_norm_w, L0_cond_k_norm_w)
    return x

_drawn_inputs = setup_inputs


def setup_inputs(seed=0):
    import zlib

    import numpy as np

    out = dict(_drawn_inputs(seed))
    spreads = {'L0_cond_q_norm_w': (1.0, 0.6), 'L0_cond_k_norm_w': (1.0, 0.6)}
    factors = {'cond_1024': 2.747,
     'L0_cond_position': 4.199,
     'L0_cond_mod_w': 2.69,
     'L0_cond_mod_b': 8.0,
     'L0_cond_w_qkv': 2.695,
     'L0_cond_w_out': 2.688}
    for name, (base, spread) in spreads.items():
        noise = np.random.default_rng([zlib.crc32(name.encode()), seed]).standard_normal(out[name].shape)
        drawn = base * np.exp(spread * noise) if base else spread * noise
        out[name] = jnp.asarray(drawn.astype(out[name].dtype))
    for name, factor in factors.items():
        out[name] = (out[name] * factor).astype(out[name].dtype)
    return out
```

```python
from contextlib import ExitStack

import concourse.bass as bass
from concourse import mybir

ALU = mybir.AluOpType
ACT = mybir.ActivationFunctionType
AX = mybir.AxisListType
F32 = mybir.dt.float32
F32R = mybir.dt.float32r
I32 = mybir.dt.int32

P = 128
PROBS_BUF = ([3, 0, 1, 2], [4, 0, 1, 2])
RSQRT_MAGIC = 0x5F3759DF


class Batch:

    def __init__(self, first, i=None):
        self.first, self.i, self.parity = first, i, first % 2

    def at(self, per, more=0):
        known = per * self.first + more
        return known if self.i is None else self.i * (2 * per) + known

    def plus(self, n):
        return Batch(self.first + n, self.i)

    def wrapped(self, n):
        return self.first % n if self.i is None else (self.i * 2 + self.first) % n


def cond_attention_kernel(nc, x, cond, position, mod_w, mod_b, w_qkv, w_out, q_norm_w, k_norm_w, out):
    NB, T, D = x.shape
    E = q_norm_w.shape[0]
    H = D // E
    TT = T // P
    DT = D // P
    HG = P // E
    NG = H // HG
    R = E // 2
    PAIRS = R // 2
    SK = 3 * E
    EPS = 1e-6
    SCALE = float(E) ** -0.5
    assert TT == 4 and DT == 4 and HG == 4 and NG == 4 and NB % 2 == 0

    mod_rows = nc.dram_tensor("mod_rows", (NB, 3 * D), F32, kind="Internal").ap()
    x_t = x.rearrange("b (t p) d -> b t p d", p=P)
    out_t = out.rearrange("b (t p) d -> b t p d", p=P)

    with ExitStack() as ctx:
        def sb(name, shape, dt=F32):
            return ctx.enter_context(nc.sbuf_tensor(name, shape, dt))

        def sem(name):
            return ctx.enter_context(nc.semaphore(name))

        wqkv_hi = sb("wqkv_hi", [P, DT, 3 * D], F32R)
        wqkv_lo = sb("wqkv_lo", [P, DT, 3 * D], F32R)
        wout = sb("wout", [P, DT, D])
        ident = sb("ident", [P, P])
        ident_r = sb("ident_r", [P, P], F32R)
        ones = sb("ones", [P, E])
        rope_same = sb("rope_same", [P, TT, 2, E])
        rope_pair = sb("rope_pair", [P, TT, 2, R])
        shift_scale = sb("shift_scale", [P, 2, D])
        gate = sb("gate", [P, D])
        xin = sb("xin", [P, 2, D])
        hT_hi = sb("hT_hi", [P, DT, P], F32R)
        hT_lo = sb("hT_lo", [P, DT, P], F32R)
        squares = sb("squares", [P, D])
        rows = sb("rows", [P, 2, TT, 2, D])
        pair_part = sb("pair_part", [P, H, R])
        vals = sb("vals", [P, 2, TT, D])
        stack = sb("stack", [P, TT, 2, SK], F32R)
        stackT = sb("stackT", [P, 2, 2, T], F32R)
        neg_max = sb("neg_max", [P, 2, TT], F32R)
        probs = sb("probs", [P, 5, TT, T])
        colsum = sb("colsum", [P, 5, T])
        oT = sb("oT", [P, 2, NG, T])
        xres = sb("xres", [P, 2, D])
        ybuf = sb("ybuf", [P, D])
        bn = sb("bn", [P, 6])
        stats = sb("stats", [P, 2 + 2 * H])
        half_var = sb("half_var", [P, 1 + 2 * H])
        rstd = sb("rstd", [P, 1 + 2 * H])
        newton = sb("newton", [P, 1 + 2 * H])

        S = ctx.enter_context(nc.psum_tensor("S", [P, 2, 512], F32))
        M = ctx.enter_context(nc.psum_tensor("M", [P, 2, 512], F32))
        TP = ctx.enter_context(nc.psum_tensor("TP", [P, 2, 512], F32))
        Q = ctx.enter_context(nc.psum_tensor("Q", [P, 512], F32))
        O = ctx.enter_context(nc.psum_tensor("O", [P, 512], F32))

        ld_w, ld_modw, ld_wout = sem("ld_w"), sem("ld_modw"), sem("ld_wout")
        ld_cond, ld_tables = sem("ld_cond"), sem("ld_tables")
        ld_x = [sem("ld_x0"), sem("ld_x1")]
        ld_res = [sem("ld_res0"), sem("ld_res1")]
        st_y = [sem("st_y0"), sem("st_y1")]
        ld_ss, ld_gate, st_mod = sem("ld_ss"), sem("ld_gate"), sem("st_mod")
        xT_done, proj_done, stackT_done, max_scores, row_done = (
            sem("xT_done"), sem("proj_done"), sem("stackT_done"), sem("max_scores"), sem("row_done"))
        scores_done, pv_done, sums_done, y_done, siluT_done, mod_done = (
            sem("scores_done"), sem("pv_done"), sem("sums_done"), sem("y_done"), sem("siluT_done"),
            sem("mod_done"))
        stackT_out, row_out, exp_done, h_hi, raw_out, v_out, sums_out, cond_exp = (
            sem("stackT_out"), sem("row_out"), sem("exp_done"), sem("h_hi"), sem("raw_out"), sem("v_out"),
            sem("sums_out"), sem("cond_exp"))
        max_out, stack_hi, stack_ready, x_stats, x_norm, h_lo = (
            sem("max_out"), sem("stack_hi"), sem("stack_ready"), sem("x_stats"), sem("x_norm"), sem("h_lo"))
        ss_done, newton_step, qk_norm, recip_done, o_ready, y_gated = (
            sem("ss_done"), sem("newton_step"), sem("qk_norm"), sem("recip_done"), sem("o_ready"),
            sem("y_gated"))
        ident_ready, silu_ready, siluT_ready, mod_ready, w_ready, tables_ready = (
            sem("ident_ready"), sem("silu_ready"), sem("siluT_ready"), sem("mod_ready"), sem("w_ready"),
            sem("tables_ready"))
        silu_step, w_step, table_step = sem("silu_step"), sem("w_step"), sem("table_step")
        h_scaled, h_rows, rope_step, sum_step, sum_rows, y_ready, consts = (
            sem("h_scaled"), sem("h_rows"), sem("rope_step"), sem("sum_step"), sem("sum_rows"),
            sem("y_ready"), sem("consts"))

        w_raw = probs[:, 0:3].rearrange("p a t q -> p (a t q)").rearrange("p (c n) -> p c n", c=DT)
        modw_raw = rows[:].rearrange("p a t j d -> p (a t j d)")[:, 0:DT * 3 * D].rearrange(
            "p (c n) -> p c n", c=DT)
        cond_sb = oT[0:NB, 0, 0, :]
        silu_sb = oT[0:NB, 0, 1, :]
        siluT = oT[:, 0, 2, 0:DT * NB].rearrange("p (c b) -> p c b", c=DT)
        modb_sb = oT[0:1, 1, 0:3, :].rearrange("p a t -> p (a t)")
        mod_sb = probs[0:NB, 3, 0:3, :]
        w_mean = colsum[:, 0, 0:DT * 2 * H].rearrange("p (c h) -> p c h", c=DT)
        pos_sb = xres[:, 0, 0:TT * R].rearrange("p (t c) -> p t c", t=TT)
        norm_w = xres[:, 1, 0:2 * E].rearrange("p (j e) -> p j e", j=2)

        def buf(h):
            return PROBS_BUF[(h // HG) % 2][h % HG]

        block = ctx.enter_context(nc.Block())

        @block.sync
        def _(sp):
            sp.dma_start(cond_sb, cond).then_inc(ld_cond, 16)
            sp.dma_start(modb_sb, mod_b.rearrange("(a n) -> a n", a=1)).then_inc(ld_cond, 16)
            sp.dma_start(pos_sb, position.rearrange("(t p) i c -> p t (i c)", p=P)).then_inc(ld_tables, 16)
            for j, w in enumerate((q_norm_w, k_norm_w)):
                sp.dma_start(norm_w[:, j, :], w.rearrange("(a e) -> a e", a=1).to_broadcast([P, E])
                             ).then_inc(ld_tables, 16)
            sp.dma_start(w_raw, w_qkv.rearrange("(c p) n -> p c n", p=P)).then_inc(ld_w, 16)
            sp.dma_start(modw_raw, mod_w.rearrange("(c p) n -> p c n", p=P)).then_inc(ld_modw, 16)
            sp.dma_start(wout[:], w_out.rearrange("(c p) n -> p c n", p=P)).then_inc(ld_wout, 16)
            for t in range(2):
                sp.dma_start(xin[:, t, :], x_t[0, t]).then_inc(ld_x[t], 16)
            sp.wait_ge(mod_ready, 3)
            sp.dma_start(mod_rows.rearrange("b (a d) -> b a d", a=3), mod_sb).then_inc(st_mod, 16)
            sp.wait_ge(st_mod, 16)

            def load_shift_scale(row):
                sp.dma_start(shift_scale[:], mod_rows[bass.ds(row, 1), 0:2 * D].rearrange(
                    "b (a d) -> b a d", a=2).to_broadcast([P, 2, D])).then_inc(ld_ss, 16)

            def load_x(batch, tile, c, b):
                sp.wait_ge(xT_done, b.at(TT, c - 1))
                sp.dma_start(xin[:, c % 2, :], x_t[bass.ds(batch, 1), tile].rearrange("b p d -> (b p) d")
                             ).then_inc(ld_x[c % 2], 16)

            load_shift_scale(0)
            b0 = Batch(0)
            for t in range(2, TT):
                load_x(0, t, t, b0)
            for t in range(2):
                load_x(1, t, TT + t, b0)
            sp.wait_ge(h_rows, TT)
            load_shift_scale(1)
            load_x(1, 2, TT + 2, b0)

            def store_and_load(b, more):
                prev = b.plus(-1)
                if b.first > 0:
                    sp.wait_ge(y_gated, prev.at(TT, 1))
                    sp.dma_start(gate[:], mod_rows[bass.ds(prev.at(1), 1), 2 * D:3 * D].to_broadcast([P, D])
                                 ).then_inc(ld_gate, 16)
                for t in range(TT):
                    if b.first > 0:
                        if b.first == 1 and t == 0:
                            sp.wait_ge(tables_ready, 1)
                        if prev.first > 0 or t >= 2:
                            sp.wait_ge(st_y[t % 2], prev.at(2 * 16, 16 * (t // 2)))
                        sp.dma_start(xres[:, t % 2, :], x_t[bass.ds(prev.at(1), 1), t].rearrange(
                            "b p d -> (b p) d")).then_inc(ld_res[t % 2], 16)
                    if more:
                        c = TT + 3 + t
                        batch = b.at(1, 1) if t == 0 else b.plus(2).wrapped(NB)
                        load_x(batch, (3 + t) % TT, c, b)
                        if t == 2:
                            sp.wait_ge(h_rows, b.at(TT, 2 * TT))
                            load_shift_scale(b.plus(2).wrapped(NB))
                    if b.first > 0:
                        sp.wait_ge(y_ready, prev.at(TT, t + 1))
                        sp.dma_start(out_t[bass.ds(prev.at(1), 1), t].rearrange("b p d -> (b p) d"),
                                     xres[:, t % 2, :]).then_inc(st_y[t % 2], 16)

            store_and_load(Batch(0), True)
            with sp.Fori(0, (NB - 2) // 2) as i:
                store_and_load(Batch(1, i), True)
                store_and_load(Batch(2, i), True)
            store_and_load(Batch(NB - 1), False)
            store_and_load(Batch(NB), False)
            for t in range(2):
                sp.wait_ge(st_y[t], 2 * 16 * NB)

        @block.tensor
        def _(pe):
            pe.wait_ge(consts, 6)
            pe.wait_ge(silu_ready, 1)
            for c in range(DT):
                mm = pe.transpose(TP[:, 0, c * NB:(c + 1) * NB], silu_sb[:, c * P:(c + 1) * P],
                                  ident[0:NB, 0:NB])
            mm.then_inc(siluT_done, 1)
            pe.wait_ge(siluT_ready, 1)
            pe.wait_ge(ld_modw, 16)
            pe.wait_ge(ld_cond, 32)
            for j, bank in enumerate((M[0:NB, 0, :], M[0:NB, 1, :], Q[0:NB, :])):
                for c in range(DT):
                    pe.matmul(bank, siluT[:, c, :], modw_raw[:, c, j * D:(j + 1) * D],
                              start=(c == 0), stop=False)
                mm = pe.matmul(bank, ones[0:1, 0:NB], modb_sb[:, j * D:(j + 1) * D], start=False, stop=True)
            mm.then_inc(mod_done, 1)
            pe.wait_ge(mod_ready, 3)
            pe.wait_ge(w_ready, 1)
            pe.wait_ge(ident_ready, 1)
            pe.wait_ge(ld_wout, 16)

            def transpose_x(b, c):
                pe.wait_ge(h_rows, b.at(TT, c + 1))
                for k in range(DT):
                    mm = pe.transpose(TP[:, 1, k * P:(k + 1) * P], xin[:, c % 2, k * P:(k + 1) * P], ident[:])
                mm.then_inc(xT_done, 1)

            def project(b, c, j):
                cols = slice(j * D, (j + 1) * D)
                terms = [(a, w, k) for k in range(DT)
                         for a, w in ((hT_hi, wqkv_hi), (hT_hi, wqkv_lo), (hT_lo, wqkv_hi))]

                def piece(n):
                    if n == 0:
                        pe.wait_ge(h_hi, b.at(TT, c + 1))
                        pe.wait_ge(h_lo, b.at(TT, c + 1))
                        if j > 0:
                            pe.wait_ge(raw_out, b.at(2 * TT, 2 * c + j))
                        elif c > 0 or b.first > 0:
                            pe.wait_ge(v_out, b.at(TT, c))
                            if b.first > 0:
                                pe.wait_ge(y_gated, b.at(TT, c - 2 * TT + 1))
                    for m in range(3 * n, 3 * n + 3):
                        a, w, k = terms[m]
                        mm = pe.matmul(Q[:], a[:, k, :], w[:, k, cols], start=(m == 0), stop=(m == 11))
                    if n == 3:
                        mm.then_inc(proj_done, 1)
                return piece

            def stack_transposes(b, h):
                pe.wait_ge(stack_ready, b.at(H, h + 1))
                if h > 0 or b.first > 0:
                    pe.wait_ge(row_out, b.at(H, h))
                for j in range(2):
                    for t in range(TT):
                        mm = pe.transpose(TP[0:SK, j, t * P:(t + 1) * P].bitcast(F32R), stack[:, t, j, :],
                                          ident_r[:])
                mm.then_inc(stackT_done, 1)

            def scores_for_max(b, h, t):
                if t == 0:
                    pe.wait_ge(stackT_out, b.at(H, h + 1))
                if h > 0 or b.first > 0 or t >= 2:
                    pe.wait_ge(max_out, b.at(TT * H, TT * h + t - 1))
                qT, kT = stackT[0:SK, h % 2, 0, :], stackT[0:SK, h % 2, 1, :]
                pe.matmul(M[:, t % 2, :], qT[:, t * P:(t + 1) * P], kT, start=True, stop=True
                          ).then_inc(max_scores, 1)

            def max_row(b, h):
                pe.wait_ge(max_out, b.at(TT * H, TT * (h + 1)))
                pe.wait_ge(stackT_out, b.at(H, h + 1))
                for t in range(TT):
                    mm = pe.transpose(TP[0:1, 0, t * P:(t + 1) * P].bitcast(F32R), neg_max[:, h % 2, t:t + 1],
                                      ident_r[:])
                mm.then_inc(row_done, 1)

            def scores(b, h, half):
                if half == 0:
                    pe.wait_ge(row_out, b.at(H, h + 1))
                if h > 0 or b.first > 0 or half:
                    pe.wait_ge(exp_done, b.at(2 * H, 2 * h + half))
                qT, kT = stackT[0:SK + 1, h % 2, 0, :], stackT[0:SK + 1, h % 2, 1, :]
                for t in range(2):
                    k = 2 * half + t
                    mm = pe.matmul(S[:, t, :], kT[:, k * P:(k + 1) * P], qT, start=True, stop=True)
                mm.then_inc(scores_done, 1)

            def weigh_values(b, g, tiles):
                if tiles[0] == 0:
                    pe.wait_ge(exp_done, b.at(2 * H, 2 * HG * (g + 1)))
                    pe.wait_ge(v_out, b.at(TT, TT))
                    if g > 0 or b.first > 0:
                        pe.wait_ge(o_ready, b.at(NG, g))
                for k in tiles:
                    for i in range(HG):
                        h = HG * g + i
                        mm = pe.matmul(O[E * i:E * (i + 1), :], vals[:, b.parity, k, E * h:E * (h + 1)],
                                       probs[:, buf(h), k, :], start=(k == 0), stop=(k == TT - 1),
                                       skip_group_check=True)
                if tiles[-1] == TT - 1:
                    mm.then_inc(pv_done, 1)

            def column_sums(b, g):
                pe.wait_ge(sum_rows, b.at(H, HG * (g + 1)))
                for i in range(HG):
                    mm = pe.matmul(TP[E * i:E * (i + 1), 1, :], ones[:, 0:E], colsum[:, buf(HG * g + i), :],
                                   start=True, stop=True, skip_group_check=True)
                mm.then_inc(sums_done, 1)

            def project_out(b, t, last):
                def piece(g):
                    if g == 0:
                        pe.wait_ge(o_ready, b.at(NG, NG))
                        if not last:
                            pe.wait_ge(v_out, b.at(TT, 2 * TT + t + 1))
                        else:
                            pe.wait_ge(y_gated, b.at(TT, t + 1))
                    mm = pe.matmul(Q[:], oT[:, b.parity, g, t * P:(t + 1) * P], wout[:, g, :],
                                   start=(g == 0), stop=(g == NG - 1))
                    if g == NG - 1:
                        mm.then_inc(y_done, 1)
                return piece

            def nothing(n):
                pass

            def body(b, has_next):
                has_prev = b.first > 0
                prev, nxt = b.plus(-1), b.plus(1)
                for h in range(H):
                    t, kind = h // 4, h % 4
                    fill = nothing
                    if kind < 3 and has_next:
                        fill = project(b, TT + t, kind)
                    elif kind == 3 and has_prev:
                        fill = project_out(prev, t, not has_next)
                    ahead = h + 1 < H or has_next
                    bb, hh = (b, h + 1) if h + 1 < H else (nxt, 0)
                    group = (b, t - 1) if t > 0 else (prev, NG - 1)
                    pv = kind == 0 and (t > 0 or has_prev)
                    max_row(b, h)
                    if pv:
                        weigh_values(*group, [0, 1])
                    else:
                        fill(0)
                    scores(b, h, 0)
                    if ahead:
                        if kind == 0 and (h == 0 or has_next):
                            pe.wait_ge(h_lo, b.at(TT, TT + t + 1))
                        if kind == 1 and (h > 1 or has_prev):
                            pe.wait_ge(sums_out, group[0].at(NG, group[1] + 1))
                        stack_transposes(bb, hh)
                    if pv:
                        weigh_values(*group, [2, 3])
                        fill(0)
                    fill(1)
                    scores(b, h, 1)
                    if ahead:
                        scores_for_max(bb, hh, 0)
                        scores_for_max(bb, hh, 1)
                    fill(2)
                    if ahead:
                        scores_for_max(bb, hh, 2)
                        scores_for_max(bb, hh, 3)
                    if kind == 3 and has_next:
                        pe.wait_ge(stackT_out, bb.at(H, hh + 1))
                        transpose_x(b, TT + t + 1)
                    fill(3)
                    if pv:
                        pe.wait_ge(stackT_out, bb.at(H, hh + 1))
                        column_sums(*group)

            b0, last = Batch(0), Batch(NB - 1)
            transpose_x(b0, 0)
            for t in range(TT):
                for j in range(3):
                    piece = project(b0, t, j)
                    for n in range(4):
                        piece(n)
                pe.wait_ge(h_lo, t + 1)
                transpose_x(b0, t + 1)
            pe.wait_ge(h_lo, TT + 1)
            stack_transposes(b0, 0)
            for t in range(TT):
                scores_for_max(b0, 0, t)
            body(b0, True)
            with pe.Fori(0, (NB - 2) // 2) as i:
                body(Batch(1, i), True)
                body(Batch(2, i), True)
            body(last, False)
            weigh_values(last, NG - 1, [0, 1, 2, 3])
            column_sums(last, NG - 1)
            for t in range(TT):
                piece = project_out(last, t, True)
                for g in range(NG):
                    piece(g)

        @block.scalar
        def _(act):
            act.wait_ge(ld_cond, 32)
            act.activation(silu_sb, cond_sb, ACT.Exp, scale=-1.0).then_inc(cond_exp, 1)

            def x_high(b, c):
                act.wait_ge(xT_done, b.at(TT, c + 1))
                if c > 0 or b.first > 0:
                    act.wait_ge(proj_done, b.at(3 * TT, 3 * c))
                act.activation(hT_hi[:].rearrange("p c t -> p (c t)"), TP[:, 1, :], ACT.Copy
                               ).then_inc(h_hi, 1)

            def evacuate(b, c, j):
                act.wait_ge(proj_done, b.at(3 * TT, 3 * c + j + 1))
                par, t = (b.first + c // TT) % 2, c % TT
                if j == 2:
                    if c >= TT and b.first > 0:
                        act.wait_ge(pv_done, b.at(NG, 0))
                    act.activation(vals[:, par, t, :], Q[:], ACT.Copy).then_inc(v_out, 1)
                    return
                if c >= TT and b.first > 0:
                    act.wait_ge(stack_ready, b.at(H, 0))
                act.activation(rows[:, par, t, j, :], Q[:], ACT.Copy)
                if c > 0 or b.first > 0 or j > 0:
                    act.wait_ge(ss_done, b.at(2 * TT, 2 * c + j))
                act.activation(squares[:], Q[:], ACT.Square, scale=SCALE).then_inc(raw_out, 1)

            def stack_out(b, h):
                act.wait_ge(stackT_done, b.at(H, h + 1))
                if h > 1 or b.first > 0:
                    act.wait_ge(scores_done, b.at(2 * H, 2 * h - 2))
                act.activation(stackT[0:SK, h % 2, :, :], TP[0:SK, :, :], ACT.Copy).then_inc(stackT_out, 1)

            def row(b, h):
                act.wait_ge(row_done, b.at(H, h + 1))
                act.activation(stackT[SK:SK + 1, h % 2, 0, :], TP[0:1, 0, :], ACT.Copy).then_inc(row_out, 1)

            def exponentials(b, h, half):
                act.wait_ge(scores_done, b.at(2 * H, 2 * h + half + 1))
                if half == 0:
                    before = h // HG - (2 if h % HG == 0 else 1)
                    if before >= 0 or b.first > 0:
                        act.wait_ge(pv_done, b.at(NG, before + 1))
                        act.wait_ge(sum_rows, b.at(H, HG * (before + 1)))
                act.activation(probs[:, buf(h), 2 * half:2 * half + 2, :], S[:], ACT.Exp, scale=SCALE
                               ).then_inc(exp_done, 1)

            def copy_sums(b, g):
                act.wait_ge(sums_done, b.at(NG, g + 1))
                if b.first > 1:
                    act.wait_ge(y_done, b.at(TT, -TT))
                act.activation(oT[:, b.parity, g, :], TP[:, 1, :], ACT.Copy).then_inc(sums_out, 1)

            def body(b, has_next):
                has_prev = b.first > 0
                prev, nxt = b.plus(-1), b.plus(1)
                for h in range(H):
                    t, kind = h // 4, h % 4
                    row(b, h)
                    exponentials(b, h, 0)
                    if h + 1 < H:
                        stack_out(b, h + 1)
                    elif has_next:
                        stack_out(nxt, 0)
                    exponentials(b, h, 1)
                    if kind < 3 and has_next:
                        evacuate(b, TT + t, kind)
                    if kind == 3 and has_next:
                        x_high(b, TT + t + 1)
                    if kind == 0 and (t > 0 or has_prev):
                        copy_sums(*((b, t - 1) if t > 0 else (prev, NG - 1)))

            b0, last = Batch(0), Batch(NB - 1)
            x_high(b0, 0)
            for t in range(TT):
                for j in range(3):
                    evacuate(b0, t, j)
                x_high(b0, t + 1)
            stack_out(b0, 0)
            body(b0, True)
            with act.Fori(0, (NB - 2) // 2) as i:
                body(Batch(1, i), True)
                body(Batch(2, i), True)
            body(last, False)
            copy_sums(last, NG - 1)

        @block.vector
        def _(dve):
            dve.sem_inc(y_gated, 1)
            dve.wait_ge(consts, 6)
            dve.tensor_copy(ident_r[:], ident[:]).then_inc(ident_ready, 1)
            dve.wait_ge(cond_exp, 1)
            dve.tensor_scalar(silu_sb, silu_sb, 1.0, None, ALU.add).then_inc(silu_step, 1)
            dve.wait_ge(silu_step, 1)
            dve.reciprocal(silu_sb, silu_sb).then_inc(silu_step, 1)
            dve.wait_ge(silu_step, 2)
            dve.tensor_tensor(silu_sb, silu_sb, cond_sb, ALU.mult).then_inc(silu_ready, 1)
            dve.wait_ge(siluT_done, 1)
            dve.tensor_copy(siluT, TP[:, 0, 0:DT * NB].rearrange("p (c b) -> p c b", c=DT)
                            ).then_inc(siluT_ready, 1)
            dve.wait_ge(ld_w, 16)
            w_qk = w_raw[:, :, 0:2 * D].rearrange("p c (h e) -> p c h e", e=E)
            dve.tensor_reduce(w_mean, w_qk, AX.X, ALU.add).then_inc(w_step, 1)
            dve.wait_ge(w_step, 1)
            dve.tensor_scalar(w_mean, w_mean, 1.0 / E, None, ALU.mult).then_inc(w_step, 1)
            dve.wait_ge(w_step, 2)
            dve.tensor_tensor(w_qk, w_qk, w_mean.unsqueeze(3).to_broadcast([P, DT, 2 * H, E]), ALU.subtract
                              ).then_inc(w_step, 1)
            dve.wait_ge(w_step, 3)
            dve.tensor_copy(wqkv_hi[:], w_raw).then_inc(w_step, 1)
            dve.wait_ge(w_step, 4)
            dve.tensor_tensor(wqkv_lo[:], w_raw, wqkv_hi[:].bitcast(F32), ALU.subtract).then_inc(w_ready, 1)
            dve.wait_ge(mod_done, 1)
            dve.tensor_copy(mod_sb[:, 0, :], M[0:NB, 0, :]).then_inc(mod_ready, 1)
            dve.tensor_scalar(mod_sb[:, 1, :], M[0:NB, 1, :], 1.0, None, ALU.add).then_inc(mod_ready, 1)
            dve.tensor_copy(mod_sb[:, 2, :], Q[0:NB, :]).then_inc(mod_ready, 1)
            dve.wait_ge(ld_tables, 16 * 3)
            for j in range(2):
                w = norm_w[:, j, 0:R].rearrange("p (i two) -> p i two", two=2)
                dve.tensor_copy(rope_same[:, :, j, R:E], norm_w[:, j, R:E].unsqueeze(1).to_broadcast([P, TT, R]))
                for t in range(TT):
                    pos = pos_sb[:, t, :].rearrange("p (i c) -> p i c", c=2)
                    dve.tensor_tensor(rope_same[:, t, j, 0:R].rearrange("p (i two) -> p i two", two=2),
                                      pos[:, :, 0:1].to_broadcast([P, PAIRS, 2]), w, ALU.mult)
                    dve.tensor_tensor(rope_pair[:, t, j, :].rearrange("p (i two) -> p i two", two=2),
                                      pos[:, :, 1:2].to_broadcast([P, PAIRS, 2]), w[:, :, ::-1], ALU.mult
                                      ).then_inc(table_step, 1)
            dve.wait_ge(table_step, 2 * TT)
            even = rope_pair[:].rearrange("p t j (i two) -> p (t j i) two", two=2)[:, :, 0:1]
            dve.tensor_scalar(even, even, -1.0, None, ALU.mult).then_inc(tables_ready, 1)
            dve.memset(stats[:], 1.0).then_inc(x_stats, 1)
            dve.wait_ge(x_stats, 1)

            NEWTON = 13

            def x_statistics(b, c):
                dve.wait_ge(ld_x[c % 2], b.at(16 * TT // 2, 16 * (c // 2 + 1)))
                if c > 0 or b.first > 0:
                    dve.wait_ge(x_stats, b.at(2 * TT, 2 * c + 1))
                dve.bn_stats(bn[:], xin[:, c % 2, :]).then_inc(x_stats, 1)

            def wait_to_aggregate(b, c):
                dve.wait_ge(x_stats, b.at(2 * TT, 2 * c + 2))
                if c > 0 or b.first > 0:
                    dve.wait_ge(x_norm, b.at(TT, c))

            def aggregate_x():
                dve.bn_aggr(stats[:, 0:2], bn[:]).then_inc(x_stats, 1)

            def square_sums(b, c, j):
                dve.wait_ge(raw_out, b.at(2 * TT, 2 * c + j + 1))
                dve.wait_ge(newton_step, b.at(NEWTON * TT, NEWTON * (c + 1)))
                dve.tensor_reduce(stats[:, 2 + j * H:2 + (j + 1) * H],
                                  squares[:].rearrange("p (h e) -> p h e", e=E), AX.X, ALU.add
                                  ).then_inc(ss_done, 1)

            def inverse_roots(b, c):
                base = NEWTON * c

                def step(n, ins):
                    ins.then_inc(newton_step, 1)
                    dve.wait_ge(newton_step, b.at(NEWTON * TT, base + n))

                dve.wait_ge(x_stats, b.at(2 * TT, 2 * c + 3))
                if c > 0 or b.first > 0:
                    dve.wait_ge(ss_done, b.at(2 * TT, 2 * c))
                    dve.wait_ge(x_norm, b.at(TT, c))
                if c > 1 or b.first > 0:
                    dve.wait_ge(qk_norm, b.at(TT, c - 1))
                step(1, dve.tensor_scalar(rstd[:], stats[:, 1:], EPS, None, ALU.add))
                step(2, dve.tensor_scalar(newton[:].bitcast(I32), rstd[:].bitcast(I32), 1, None,
                                          ALU.logical_shift_right))
                step(3, dve.tensor_scalar(half_var[:], rstd[:], -0.5, None, ALU.mult))
                step(4, dve.tensor_scalar(rstd[:].bitcast(I32), newton[:].bitcast(I32), -1.0,
                                          float(RSQRT_MAGIC), ALU.mult, ALU.add))
                for n in range(3):
                    step(5 + 3 * n, dve.tensor_tensor(newton[:], rstd[:], rstd[:], ALU.mult))
                    step(6 + 3 * n, dve.tensor_tensor(newton[:], newton[:], half_var[:], ALU.mult))
                    step(7 + 3 * n, dve.scalar_tensor_tensor(rstd[:], newton[:], 1.5, rstd[:], ALU.add,
                                                             ALU.mult))

            def normalize_x(b, c):
                xt = xin[:, c % 2, :]
                dve.tensor_scalar(xt, xt, stats[:, 0:1], rstd[:, 0:1], ALU.subtract, ALU.mult
                                  ).then_inc(x_norm, 1)

            def normalize_qk(b, c):
                par = (b.first + c // TT) % 2
                qk = rows[:, par, c % TT, :, :].rearrange("p j (h e) -> p (j h) e", e=E)
                dve.tensor_tensor(qk, qk, rstd[:, 1:].unsqueeze(2).to_broadcast([P, 2 * H, E]), ALU.mult
                                  ).then_inc(qk_norm, 1)

            def x_low(b, c):
                dve.wait_ge(h_hi, b.at(TT, c + 1))
                dve.tensor_tensor(hT_lo[:].rearrange("p c t -> p (c t)"), TP[:, 1, :],
                                  hT_hi[:].rearrange("p c t -> p (c t)").bitcast(F32), ALU.subtract
                                  ).then_inc(h_lo, 1)

            def stack_at(offset, j_step):
                whole = stack[:]
                return bass.AP(tensor=whole.tensor, offset=whole.offset + offset,
                               ap=[whole.ap[0], [2 * SK, TT], [j_step, 2], [1, E]])

            def make_stack(b, h):
                if h == 0:
                    dve.wait_ge(rope_step, b.at(6 * TT, 6 * TT))
                if h > 0 or b.first > 0:
                    dve.wait_ge(stackT_done, b.at(H, h))
                src = rows[:, b.parity, :, :, h * E:(h + 1) * E]
                dve.tensor_copy(stack_at(0, SK), src).then_inc(stack_hi, 1)
                dve.tensor_copy(stack_at(E, SK + E), src).then_inc(stack_hi, 1)
                dve.wait_ge(stack_hi, b.at(2 * H, 2 * h + 1))
                dve.tensor_tensor(stack_at(2 * E, SK - E), src, stack_at(0, SK).bitcast(F32), ALU.subtract
                                  ).then_inc(stack_ready, 1)

            def maxima(b, h):
                for t in range(TT):
                    dve.wait_ge(max_scores, b.at(TT * H, TT * h + t + 1))
                    if t == 0 and (h > 1 or b.first > 0):
                        dve.wait_ge(row_done, b.at(H, h - 1))
                    dve.tensor_reduce(neg_max[:, h % 2, t:t + 1], M[:, t % 2, :], AX.X, ALU.max, negate=True
                                      ).then_inc(max_out, 1)

            def normalize_o(b, g):
                dve.wait_ge(sums_out, b.at(NG, g + 1))
                dve.wait_ge(pv_done, b.at(NG, g + 1))
                o = oT[:, b.parity, g, :]
                dve.reciprocal(o, o).then_inc(recip_done, 1)
                dve.wait_ge(recip_done, b.at(NG, g + 1))
                dve.tensor_tensor(o, O[:], o, ALU.mult).then_inc(o_ready, 1)

            def apply_gate(b, t):
                dve.wait_ge(y_done, b.at(TT, t + 1))
                if t == 0:
                    dve.wait_ge(ld_gate, b.at(16, 16))
                if t > 0 or b.first > 0:
                    dve.wait_ge(y_ready, b.at(TT, t))
                dve.tensor_tensor(ybuf[:], Q[:], gate[:], ALU.mult).then_inc(y_gated, 1)

            def body(b, has_next):
                has_prev = b.first > 0
                prev, nxt = b.plus(-1), b.plus(1)
                for h in range(H):
                    t, kind = h // 4, h % 4
                    c = TT + t
                    if h + 1 < H or has_next:
                        bb, hh = (b, h + 1) if h + 1 < H else (nxt, 0)
                        make_stack(bb, hh)
                        maxima(bb, hh)
                    if kind == 0 and has_next:
                        x_statistics(b, c + 1)
                        wait_to_aggregate(b, c + 1)
                        square_sums(b, c, 0)
                        aggregate_x()
                    if kind == 0 and (t > 0 or has_prev):
                        normalize_o(*((b, t - 1) if t > 0 else (prev, NG - 1)))
                    if kind == 1 and has_next:
                        square_sums(b, c, 1)
                        inverse_roots(b, c + 1)
                        normalize_x(b, c + 1)
                        normalize_qk(b, c)
                    if kind == 3 and has_next:
                        x_low(b, c + 1)
                    if kind == 3 and has_prev:
                        apply_gate(prev, t)

            b0, last = Batch(0), Batch(NB - 1)
            x_statistics(b0, 0)
            wait_to_aggregate(b0, 0)
            aggregate_x()
            inverse_roots(b0, 0)
            normalize_x(b0, 0)
            x_low(b0, 0)
            for t in range(TT):
                x_statistics(b0, t + 1)
                wait_to_aggregate(b0, t + 1)
                square_sums(b0, t, 0)
                aggregate_x()
                square_sums(b0, t, 1)
                inverse_roots(b0, t + 1)
                normalize_x(b0, t + 1)
                normalize_qk(b0, t)
                x_low(b0, t + 1)
            make_stack(b0, 0)
            maxima(b0, 0)
            body(b0, True)
            with dve.Fori(0, (NB - 2) // 2) as i:
                body(Batch(1, i), True)
                body(Batch(2, i), True)
            body(last, False)
            normalize_o(last, NG - 1)
            for t in range(TT):
                apply_gate(last, t)

        @block.gpsimd
        def _(pool):
            pool.memset(ident[:], 0.0).then_inc(consts, 1)
            pool.wait_ge(consts, 1)
            pool.memset(ones[:], 1.0).then_inc(consts, 1)
            for n in range(2):
                pool.wait_ge(consts, 2 + n)
                pool.memset(stackT[SK:SK + 1, n, 1, :].bitcast(F32), 1.0).then_inc(consts, 1)
            pool.wait_ge(consts, 4)
            pool.affine_select(out=ident[:], in_=ident[:], compare_op=ALU.not_equal, fill=1.0, base=0,
                               pattern=[[-1, P]], channel_multiplier=1).then_inc(consts, 2)

            def modulate(b, c):
                pool.wait_ge(x_norm, b.at(TT, c + 1))
                pool.wait_ge(ld_ss, b.at(16, 16 * (c // TT + 1)))
                xt = xin[:, c % 2, :]
                pool.tensor_tensor(xt, xt, shift_scale[:, 1, :], ALU.mult).then_inc(h_scaled, 1)
                pool.wait_ge(h_scaled, b.at(TT, c + 1))
                pool.tensor_tensor(xt, xt, shift_scale[:, 0, :], ALU.add).then_inc(h_rows, 1)

            def rotate(b, c):
                pool.wait_ge(qk_norm, b.at(TT, c + 1))
                par, t = (b.first + c // TT) % 2, c % TT
                for j in range(2):
                    n = 6 * c + 3 * j
                    r = rows[:, par, t, j, :].rearrange("p (h e) -> p h e", e=E)
                    swapped = bass.AP(tensor=r.tensor, offset=r.offset + 1,
                                      ap=[r.ap[0], [E, H], [2, PAIRS], [-1, 2]])
                    if n > 0 or b.first > 0:
                        pool.wait_ge(rope_step, b.at(6 * TT, n))
                    pool.tensor_tensor(pair_part[:].rearrange("p h (i two) -> p h i two", two=2), swapped,
                                       rope_pair[:, t, j, :].rearrange("p (i two) -> p i two", two=2)
                                       .unsqueeze(1).to_broadcast([P, H, PAIRS, 2]), ALU.mult
                                       ).then_inc(rope_step, 1)
                    pool.wait_ge(rope_step, b.at(6 * TT, n + 1))
                    pool.tensor_tensor(r, r, rope_same[:, t, j, :].unsqueeze(1).to_broadcast([P, H, E]),
                                       ALU.mult).then_inc(rope_step, 1)
                    pool.wait_ge(rope_step, b.at(6 * TT, n + 2))
                    last = pool.tensor_tensor(r[:, :, 0:R], r[:, :, 0:R], pair_part[:], ALU.add)
                    last.then_inc(rope_step, 1)

            def sum_key_tiles(b, h):
                n = buf(h)
                before = h // HG - (2 if h % HG == 0 else 1)
                pool.wait_ge(exp_done, b.at(2 * H, 2 * h + 1))
                if before >= 0 or b.first > 0:
                    pool.wait_ge(sums_done, b.at(NG, before + 1))
                pool.tensor_tensor(colsum[:, n, :], probs[:, n, 0, :], probs[:, n, 1, :], ALU.add
                                   ).then_inc(sum_step, 1)
                pool.wait_ge(sum_step, b.at(2 * H, 2 * h + 1))
                pool.wait_ge(exp_done, b.at(2 * H, 2 * h + 2))
                pool.tensor_tensor(colsum[:, n, :], colsum[:, n, :], probs[:, n, 2, :], ALU.add
                                   ).then_inc(sum_step, 1)
                pool.wait_ge(sum_step, b.at(2 * H, 2 * h + 2))
                pool.tensor_tensor(colsum[:, n, :], colsum[:, n, :], probs[:, n, 3, :], ALU.add
                                   ).then_inc(sum_rows, 1)

            def add_residual(b, t):
                pool.wait_ge(y_gated, b.at(TT, t + 2))
                pool.wait_ge(ld_res[t % 2], b.at(32, 16 * (t // 2 + 1)))
                r = xres[:, t % 2, :]
                pool.tensor_tensor(r, r, ybuf[:], ALU.add).then_inc(y_ready, 1)

            def body(b, has_next):
                prev = b.plus(-1)
                for h in range(H):
                    t, kind = h // 4, h % 4
                    if kind == 2 and has_next:
                        modulate(b, TT + t + 1)
                        rotate(b, TT + t)
                    sum_key_tiles(b, h)
                    if kind == 3 and b.first > 0:
                        add_residual(prev, t)

            b0, last = Batch(0), Batch(NB - 1)
            pool.wait_ge(tables_ready, 1)
            modulate(b0, 0)
            for t in range(TT):
                modulate(b0, t + 1)
                rotate(b0, t)
            body(b0, True)
            with pool.Fori(0, (NB - 2) // 2) as i:
                body(Batch(1, i), True)
                body(Batch(2, i), True)
            body(last, False)
            for t in range(TT):
                add_residual(last, t)


_INS = ["x", "cond_1024", "L0_cond_position", "L0_cond_mod_w", "L0_cond_mod_b", "L0_cond_w_qkv",
        "L0_cond_w_out", "L0_cond_q_norm_w", "L0_cond_k_norm_w"]


def kernel(**inputs):
    import numpy as _np
    import concourse.bacc as _bacc
    from concourse import mybir as _mybir
    from concourse.bass_utils import run_bass_kernel_spmd as _run

    nc = _bacc.Bacc("TRN2", target_bir_lowering=False, num_devices=1)
    arrays, args = {}, []
    for name in _INS:
        a = _np.ascontiguousarray(inputs[name])
        arrays[f"in_{name}_dram"] = a
        args.append(nc.dram_tensor(f"in_{name}_dram", a.shape, _mybir.dt.from_np(a.dtype),
                                   kind="ExternalInput").ap())
    shape = tuple(inputs["x"].shape)
    args.append(nc.dram_tensor("out_0_dram", shape, _mybir.dt.float32, kind="ExternalOutput").ap())
    cond_attention_kernel(nc, *args)
    r = _run(nc, [arrays], core_ids=[0])
    return r.results[0]["out_0_dram"]
```

```python
from contextlib import ExitStack

import concourse.bass as bass
from concourse import mybir

ALU = mybir.AluOpType
ACT = mybir.ActivationFunctionType
AX = mybir.AxisListType
F32 = mybir.dt.float32
F32R = mybir.dt.float32r
I32 = mybir.dt.int32

P = 128
PROBS_BUF = ([3, 0, 1, 2], [4, 0, 1, 2])
FILL_PV, FILL_Q, FILL_K, FILL_V, FILL_OUT = (0, 1, 1, 2), (0, 1, 1, 2), (2, 2, 3, 4), (1, 2, 2, 2), (0, 1, 1, 2)
RSQRT_MAGIC = 0x5F3759DF


class Batch:

    def __init__(self, first, i=None):
        self.first, self.i, self.parity = first, i, first % 2

    def at(self, per, more=0):
        known = per * self.first + more
        return known if self.i is None else self.i * (2 * per) + known

    def plus(self, n):
        return Batch(self.first + n, self.i)

    def wrapped(self, n):
        return self.first % n if self.i is None else (self.i * 2 + self.first) % n


def cond_attention_kernel(nc, x, cond, position, mod_w, mod_b, w_qkv, w_out, q_norm_w, k_norm_w, out):
    NB, T, D = x.shape
    E = q_norm_w.shape[0]
    H = D // E
    TT = T // P
    DT = D // P
    HG = P // E
    NG = H // HG
    R = E // 2
    PAIRS = R // 2
    SK = 3 * E
    EPS = 1e-6
    SCALE = float(E) ** -0.5
    assert TT == 4 and DT == 4 and HG == 4 and NG == 4 and NB % 2 == 0

    gate_rows = nc.dram_tensor("gate_rows", (NB, D), F32, kind="Internal").ap()
    mod_cols = nc.dram_tensor("mod_cols", (NB, P, 2 * DT), F32, kind="Internal").ap()
    x_t = x.rearrange("b (t p) d -> b t p d", p=P)
    out_t = out.rearrange("b (t p) d -> b t p d", p=P)

    with ExitStack() as ctx:
        def sb(name, shape, dt=F32):
            return ctx.enter_context(nc.sbuf_tensor(name, shape, dt))

        def sem(name):
            return ctx.enter_context(nc.semaphore(name))

        wqkv_hi = sb("wqkv_hi", [P, DT, 3 * D], F32R)
        wqkv_lo = sb("wqkv_lo", [P, DT, 3 * D], F32R)
        wout = sb("wout", [P, DT, D])
        ident = sb("ident", [P, P])
        ident_r = sb("ident_r", [P, P], F32R)
        ones = sb("ones", [P, E])
        rope_same = sb("rope_same", [P, TT, 2, E])
        rope_pair = sb("rope_pair", [P, TT, 2, R])
        shift_scale = sb("shift_scale", [P, 2, 2 * DT])
        gate = sb("gate", [P, D])
        xin = sb("xin", [P, 2, D])
        hT = sb("hT", [P, DT, P])
        hT_hi = sb("hT_hi", [P, DT, P], F32R)
        hT_lo = sb("hT_lo", [P, DT, P], F32R)
        squares = sb("squares", [P, D])
        rows = sb("rows", [P, 2, TT, 2, D])
        pair_part = sb("pair_part", [P, H, R])
        vals = sb("vals", [P, 2, TT, D])
        stack = sb("stack", [P, TT, 2, SK], F32R)
        stackT = sb("stackT", [P, 2, 2, T], F32R)
        neg_max = sb("neg_max", [P, 2, TT], F32R)
        probs = sb("probs", [P, 5, TT, T])
        colsum = sb("colsum", [P, 5, T])
        oT = sb("oT", [P, 2, NG, T])
        xres = sb("xres", [P, 2, D])
        gated = sb("gated", [P, D])
        sums = sb("sums", [P, T])
        bn = sb("bn", [P, 6])
        stats = sb("stats", [P, 2 + 2 * H])
        half_var = sb("half_var", [P, 1 + 2 * H])
        rstd = sb("rstd", [P, 1 + 2 * H])
        newton = sb("newton", [P, 1 + 2 * H])

        S = ctx.enter_context(nc.psum_tensor("S", [P, 2, 512], F32))
        M = ctx.enter_context(nc.psum_tensor("M", [P, 2, 512], F32))
        TP = ctx.enter_context(nc.psum_tensor("TP", [P, 2, 512], F32))
        Q = ctx.enter_context(nc.psum_tensor("Q", [P, 512], F32))
        O = ctx.enter_context(nc.psum_tensor("O", [P, 512], F32))

        ld_w, ld_modw, ld_wout = sem("ld_w"), sem("ld_modw"), sem("ld_wout")
        ld_cond, ld_tables = sem("ld_cond"), sem("ld_tables")
        ld_x = [sem("ld_x0"), sem("ld_x1")]
        ld_res = [sem("ld_res0"), sem("ld_res1")]
        st_y = [sem("st_y0"), sem("st_y1")]
        ld_ss, ld_gate, st_mod = sem("ld_ss"), sem("ld_gate"), sem("st_mod")
        xT_done, proj_done, stackT_done, max_scores, row_done = (
            sem("xT_done"), sem("proj_done"), sem("stackT_done"), sem("max_scores"), sem("row_done"))
        scores_done, pv_done, sums_done, y_done, siluT_done, mod_done = (
            sem("scores_done"), sem("pv_done"), sem("sums_done"), sem("y_done"), sem("siluT_done"),
            sem("mod_done"))
        stackT_out, row_out, exp_done, h_ready, raw_out, v_out, o_out, sums_out, cond_exp = (
            sem("stackT_out"), sem("row_out"), sem("exp_done"), sem("h_ready"), sem("raw_out"), sem("v_out"),
            sem("o_out"), sem("sums_out"), sem("cond_exp"))
        max_out, stack_hi, stack_ready, x_stats, x_norm, h_hi, h_lo = (
            sem("max_out"), sem("stack_hi"), sem("stack_ready"), sem("x_stats"), sem("x_norm"), sem("h_hi"),
            sem("h_lo"))
        ss_done, newton_step, qk_norm, recip_done, o_ready, y_gated = (
            sem("ss_done"), sem("newton_step"), sem("qk_norm"), sem("recip_done"), sem("o_ready"),
            sem("y_gated"))
        ident_ready, silu_ready, siluT_ready, mod_ready, w_ready, tables_ready = (
            sem("ident_ready"), sem("silu_ready"), sem("siluT_ready"), sem("mod_ready"), sem("w_ready"),
            sem("tables_ready"))
        silu_step, w_step, table_step = sem("silu_step"), sem("w_step"), sem("table_step")
        rope_step, sum_step, sum_rows, y_ready, consts = (
            sem("rope_step"), sem("sum_step"), sem("sum_rows"),
            sem("y_ready"), sem("consts"))

        w_raw = probs[:, 0:3].rearrange("p a t q -> p (a t q)").rearrange("p (c n) -> p c n", c=DT)
        modw_raw = rows[:].rearrange("p a t j d -> p (a t j d)")[:, 0:DT * 3 * D].rearrange(
            "p (c n) -> p c n", c=DT)
        cond_sb = oT[0:NB, 0, 0, :]
        silu_sb = oT[0:NB, 0, 1, :]
        siluT = oT[:, 0, 2, 0:DT * NB].rearrange("p (c b) -> p c b", c=DT)
        modb_sb = oT[0:1, 1, 0:3, :].rearrange("p a t -> p (a t)")
        gate_sb = probs[0:NB, 3, 0, :]
        ss_sb = oT[:, 0, 3, 0:NB * 2 * DT].rearrange("p (b m) -> p b m", b=NB)
        w_mean = colsum[:, 0, 0:DT * 2 * H].rearrange("p (c h) -> p c h", c=DT)
        pos_sb = xres[:, 0, 0:TT * R].rearrange("p (t c) -> p t c", t=TT)
        norm_w = xres[:, 1, 0:2 * E].rearrange("p (j e) -> p j e", j=2)

        def buf(h):
            return PROBS_BUF[(h // HG) % 2][h % HG]

        def stack_at(offset, j_step):
            whole = stack[:]
            return bass.AP(tensor=whole.tensor, offset=whole.offset + offset,
                           ap=[whole.ap[0], [2 * SK, TT], [j_step, 2], [1, E]])

        block = ctx.enter_context(nc.Block())

        @block.sync
        def _(sp):
            sp.dma_start(cond_sb, cond).then_inc(ld_cond, 16)
            sp.dma_start(modb_sb, mod_b.rearrange("(a n) -> a n", a=1)).then_inc(ld_cond, 16)
            sp.dma_start(pos_sb, position.rearrange("(t p) i c -> p t (i c)", p=P)).then_inc(ld_tables, 16)
            for j, w in enumerate((q_norm_w, k_norm_w)):
                sp.dma_start(norm_w[:, j, :], w.rearrange("(a e) -> a e", a=1).to_broadcast([P, E])
                             ).then_inc(ld_tables, 16)
            sp.dma_start(w_raw, w_qkv.rearrange("(c p) n -> p c n", p=P)).then_inc(ld_w, 16)
            sp.dma_start(modw_raw, mod_w.rearrange("(c p) n -> p c n", p=P)).then_inc(ld_modw, 16)
            sp.dma_start(wout[:], w_out.rearrange("(c p) n -> p c n", p=P)).then_inc(ld_wout, 16)
            for t in range(2):
                sp.dma_start(xin[:, t, :], x_t[0, t]).then_inc(ld_x[t], 16)
            sp.wait_ge(mod_ready, 4)
            sp.dma_start(gate_rows, gate_sb).then_inc(st_mod, 16)
            sp.dma_start(mod_cols.rearrange("b p m -> p b m"), ss_sb).then_inc(st_mod, 16)

            def load_x(batch, tile, c, b):
                sp.wait_ge(xT_done, b.at(TT, c - 1))
                sp.dma_start(xin[:, c % 2, :], x_t[bass.ds(batch, 1), tile].rearrange("b p d -> (b p) d")
                             ).then_inc(ld_x[c % 2], 16)

            b0 = Batch(0)
            for t in range(2, TT):
                load_x(0, t, t, b0)
            for t in range(2):
                load_x(1, t, TT + t, b0)
            load_x(1, 2, TT + 2, b0)
            sp.wait_ge(st_mod, 32)

            def store_and_load(b, more):
                prev = b.plus(-1)
                if more:
                    sp.wait_ge(h_ready, b.at(TT, TT))
                    sp.dma_start(shift_scale[:, b.parity, :],
                                 mod_cols[bass.ds(b.plus(2).wrapped(NB), 1)].rearrange("b p m -> (b p) m")
                                 ).then_inc(ld_ss, 16)
                if b.first > 0:
                    sp.wait_ge(y_gated, prev.at(TT, 1))
                    sp.dma_start(gate[:], gate_rows[bass.ds(prev.at(1), 1)].to_broadcast([P, D])
                                 ).then_inc(ld_gate, 16)
                for t in range(TT):
                    if b.first > 0:
                        if b.first == 1 and t == 0:
                            sp.wait_ge(tables_ready, 1)
                        if prev.first > 0 or t >= 2:
                            sp.wait_ge(st_y[t % 2], prev.at(2 * 16, 16 * (t // 2)))
                        sp.dma_start(xres[:, t % 2, :], x_t[bass.ds(prev.at(1), 1), t].rearrange(
                            "b p d -> (b p) d")).then_inc(ld_res[t % 2], 16)
                    if more:
                        batch = b.at(1, 1) if t == 0 else b.plus(2).wrapped(NB)
                        load_x(batch, (3 + t) % TT, TT + 3 + t, b)
                    if b.first > 0:
                        sp.wait_ge(y_ready, prev.at(TT, t + 2))
                        sp.dma_start(out_t[bass.ds(prev.at(1), 1), t].rearrange("b p d -> (b p) d"),
                                     xres[:, t % 2, :]).then_inc(st_y[t % 2], 16)

            store_and_load(Batch(0), True)
            with sp.Fori(0, (NB - 2) // 2) as i:
                store_and_load(Batch(1, i), True)
                store_and_load(Batch(2, i), True)
            store_and_load(Batch(NB - 1), False)
            store_and_load(Batch(NB), False)
            for t in range(2):
                sp.wait_ge(st_y[t], 2 * 16 * NB)

        @block.tensor
        def _(pe):
            pe.wait_ge(consts, 6)
            pe.wait_ge(silu_ready, 1)
            for c in range(DT):
                mm = pe.transpose(TP[:, 0, c * NB:(c + 1) * NB], silu_sb[:, c * P:(c + 1) * P],
                                  ident[0:NB, 0:NB])
            mm.then_inc(siluT_done, 1)
            pe.wait_ge(siluT_ready, 1)
            pe.wait_ge(ld_modw, 16)
            pe.wait_ge(ld_cond, 32)
            for m in range(2 * DT):
                cols = slice(m * P, (m + 1) * P)
                for c in range(DT):
                    pe.matmul(M[:, 0, m * NB:(m + 1) * NB], modw_raw[:, c, cols], siluT[:, c, :],
                              start=(c == 0), stop=False)
                pe.matmul(M[:, 0, m * NB:(m + 1) * NB], modb_sb[:, cols], ones[0:1, 0:NB], start=False, stop=True)
            cols = slice(2 * D, 3 * D)
            for c in range(DT):
                pe.matmul(Q[0:NB, :], siluT[:, c, :], modw_raw[:, c, cols], start=(c == 0), stop=False)
            pe.matmul(Q[0:NB, :], ones[0:1, 0:NB], modb_sb[:, cols], start=False, stop=True).then_inc(mod_done, 1)
            pe.wait_ge(mod_ready, 4)
            pe.wait_ge(w_ready, 1)
            pe.wait_ge(ident_ready, 1)
            pe.wait_ge(ld_wout, 16)

            def transpose_x(b, c):
                pe.wait_ge(x_norm, b.at(TT, c + 1))
                for k in range(DT):
                    mm = pe.transpose(TP[:, 1, k * P:(k + 1) * P], xin[:, c % 2, k * P:(k + 1) * P], ident[:])
                mm.then_inc(xT_done, 1)

            def project(b, c, j):
                cols = slice(j * D, (j + 1) * D)
                terms = [(a, w, k) for k in range(DT)
                         for a, w in ((hT_hi, wqkv_hi), (hT_hi, wqkv_lo), (hT_lo, wqkv_hi))]

                bank = O if j == 1 else Q

                def piece(n):
                    if n == 0 and j == 0:
                        pe.wait_ge(h_lo, b.at(TT, c + 1))
                        if c > 0 or b.first > 0:
                            pe.wait_ge(v_out, b.at(TT, c))
                    if n == 0 and j == 1:
                        if c > 0 or b.first > 0:
                            pe.wait_ge(raw_out, b.at(2 * TT, 2 * c))
                        if c > TT + 1 or b.first > 0:
                            pe.wait_ge(o_out, b.at(NG, c - TT - 1))
                    if n == 0 and j == 2:
                        pe.wait_ge(raw_out, b.at(2 * TT, 2 * c + 1))
                    for m in range(3 * n, 3 * n + 3):
                        a, w, k = terms[m]
                        mm = pe.matmul(bank[:], a[:, k, :], w[:, k, cols], start=(m == 0), stop=(m == 11))
                    if n == 3:
                        mm.then_inc(proj_done, 1)
                return piece

            def stack_transposes(b, h):
                pe.wait_ge(stack_ready, b.at(H, h + 1))
                if h > 1 or b.first > 0:
                    pe.wait_ge(row_out, b.at(H, h - 1))
                for j in range(2):
                    for t in range(TT):
                        mm = pe.transpose(TP[0:SK, j, t * P:(t + 1) * P].bitcast(F32R), stack[:, t, j, :],
                                          ident_r[:])
                mm.then_inc(stackT_done, 1)

            def scores_for_max(b, h, t):
                if t == 0:
                    pe.wait_ge(stackT_out, b.at(H, h + 1))
                if h > 0 or b.first > 0 or t >= 2:
                    pe.wait_ge(max_out, b.at(TT * H, TT * h + t - 1))
                qT, kT = stackT[0:SK, h % 2, 0, :], stackT[0:SK, h % 2, 1, :]
                pe.matmul(M[:, t % 2, :], qT[:, t * P:(t + 1) * P], kT, start=True, stop=True
                          ).then_inc(max_scores, 1)

            def max_row(b, h, stacks):
                pe.wait_ge(max_out, b.at(TT * H, TT * (h + 1)))
                pe.wait_ge(stackT_out, b.at(H, stacks))
                for t in range(TT):
                    mm = pe.transpose(TP[0:1, 0, t * P:(t + 1) * P].bitcast(F32R), neg_max[:, h % 2, t:t + 1],
                                      ident_r[:])
                mm.then_inc(row_done, 1)

            def scores(b, h, half):
                if half == 0:
                    pe.wait_ge(row_out, b.at(H, h + 1))
                if h > 0 or b.first > 0 or half:
                    pe.wait_ge(exp_done, b.at(2 * H, 2 * h + half))
                qT, kT = stackT[0:SK + 1, h % 2, 0, :], stackT[0:SK + 1, h % 2, 1, :]
                for t in range(2):
                    k = 2 * half + t
                    mm = pe.matmul(S[:, t, :], kT[:, k * P:(k + 1) * P], qT, start=True, stop=True)
                mm.then_inc(scores_done, 1)

            def weigh_values(b, g, k, has_next=True):
                if k == 0:
                    pe.wait_ge(exp_done, b.at(2 * H, 2 * HG * (g + 1)))
                    pe.wait_ge(v_out, b.at(TT, TT))
                    if has_next:
                        pe.wait_ge(raw_out, b.at(2 * TT, 2 * (TT + 1 + g) + 2))
                    if b.first > 0 or g == NG - 1:
                        pe.wait_ge(y_gated, b.at(TT, g - TT + 2))
                for i in range(HG):
                    h = HG * g + i
                    mm = pe.matmul(O[E * i:E * (i + 1), :], vals[:, b.parity, k, E * h:E * (h + 1)],
                                   probs[:, buf(h), k, :], start=(k == 0), stop=(k == TT - 1),
                                   skip_group_check=True)
                if k == TT - 1:
                    mm.then_inc(pv_done, 1)

            def column_sums(b, g):
                pe.wait_ge(sum_rows, b.at(H, HG * (g + 1)))
                for i in range(HG):
                    mm = pe.matmul(TP[E * i:E * (i + 1), 1, :], ones[:, 0:E], colsum[:, buf(HG * g + i), :],
                                   start=True, stop=True, skip_group_check=True)
                mm.then_inc(sums_done, 1)

            def project_out(b, t, last, last_group=2 * NG):
                def piece(g):
                    if g == 0:
                        pe.wait_ge(o_ready, b.at(NG, NG))
                        if not last:
                            pe.wait_ge(raw_out, b.at(2 * TT, 2 * (2 * TT + 1 + t) + 2))
                        else:
                            pe.wait_ge(o_out, b.at(NG, min(NG + t, last_group)))
                            pe.wait_ge(y_gated, b.at(TT, t + 1))
                    mm = pe.matmul(O[:], oT[:, b.parity, g, t * P:(t + 1) * P], wout[:, g, :],
                                   start=(g == 0), stop=(g == NG - 1))
                    if g == NG - 1:
                        mm.then_inc(y_done, 1)
                return piece

            def body(b, has_next):
                has_prev = b.first > 0
                prev, nxt = b.plus(-1), b.plus(1)
                for h in range(H):
                    t, kind = h // 4, h % 4
                    c = TT + 1 + t
                    group = (b, t - 1) if t > 0 else (prev, NG - 1)
                    grouped = t > 0 or has_prev
                    one, two = h + 1 < H or has_next, h + 2 < H or has_next
                    head1 = (b, h + 1) if h + 1 < H else (nxt, 0)
                    head2 = (b, h + 2) if h + 2 < H else (nxt, h + 2 - H)
                    laid = []
                    if kind == 0 and grouped:
                        laid = [(FILL_PV[k], weigh_values, (*group, k, has_next or t == 0)) for k in range(TT)]
                        laid.append((2, column_sums, group))
                    if kind == 1 and has_next:
                        laid = [(FILL_Q[n], project(b, c, 0), (n,)) for n in range(4)]
                        laid += [(FILL_K[n], project(b, c, 1), (n,)) for n in range(4) if FILL_K[n] < 3]
                    if kind == 2 and has_next:
                        laid = [(FILL_K[n] - 3, project(b, c, 1), (n,)) for n in range(4) if FILL_K[n] >= 3]
                        laid += [(FILL_V[n], project(b, c, 2), (n,)) for n in range(4)]
                    if kind == 3 and has_prev:
                        laid = [(FILL_OUT[n], project_out(prev, t, not has_next), (n,)) for n in range(4)]
                    if kind == 3 and has_next:
                        laid.append((2, transpose_x, (b, c + 1)))

                    def lay(n):
                        for place, step, args in laid:
                            if place == n:
                                step(*args)

                    scores(b, h, 0)
                    if one:
                        scores_for_max(*head1, 0)
                        scores_for_max(*head1, 1)
                    lay(0)
                    scores(b, h, 1)
                    if two:
                        if kind == 0 and (has_next or t == 0):
                            pe.wait_ge(h_ready, b.at(TT, c + 1))
                        if kind == 1 and grouped:
                            pe.wait_ge(sums_out, group[0].at(NG, group[1] + 1))
                        stack_transposes(*head2)
                    if one:
                        scores_for_max(*head1, 2)
                        scores_for_max(*head1, 3)
                    lay(1)
                    if one:
                        max_row(*head1, head1[1] + (2 if two else 1))
                    lay(2)

            b0, last = Batch(0), Batch(NB - 1)
            transpose_x(b0, 0)
            for c in range(TT + 1):
                for j in range(3):
                    piece = project(b0, c, j)
                    for n in range(4):
                        piece(n)
                    if j == 0:
                        pe.wait_ge(h_ready, c + 1)
                        transpose_x(b0, c + 1)
            pe.wait_ge(h_ready, TT + 2)
            stack_transposes(b0, 0)
            pe.wait_ge(stackT_out, 1)
            stack_transposes(b0, 1)
            for t in range(TT):
                scores_for_max(b0, 0, t)
            max_row(b0, 0, 2)
            body(b0, True)
            with pe.Fori(0, (NB - 2) // 2) as i:
                body(Batch(1, i), True)
                body(Batch(2, i), True)
            body(last, False)
            for k in range(TT):
                weigh_values(last, NG - 1, k, False)
            column_sums(last, NG - 1)
            for t in range(TT):
                piece = project_out(last, t, True, NG)
                for g in range(NG):
                    piece(g)

        @block.scalar
        def _(act):
            act.wait_ge(ld_cond, 32)
            act.activation(silu_sb, cond_sb, ACT.Exp, scale=-1.0).then_inc(cond_exp, 1)

            def modulate(b, c):
                par = (b.first + c // TT) % 2
                if c == 2 * TT:
                    act.wait_ge(ld_ss, b.at(16, 16))
                act.wait_ge(xT_done, b.at(TT, c + 1))
                if c > 0 or b.first > 0:
                    act.wait_ge(h_lo, b.at(TT, c))
                for k in range(DT):
                    last = act.activation(hT[:, k, :], TP[:, 1, k * P:(k + 1) * P], ACT.Identity,
                                          bias=shift_scale[:, par, k:k + 1],
                                          scale=shift_scale[:, par, DT + k:DT + k + 1])
                last.then_inc(h_ready, 1)

            def move_out(b, c, j):
                act.wait_ge(proj_done, b.at(3 * TT, 3 * c + j + 1))
                par, t = (b.first + c // TT) % 2, c % TT
                if j == 2:
                    if t == 0 and b.first > 0:
                        act.wait_ge(pv_done, b.at(NG, 0))
                    act.activation(vals[:, par, t, :], Q[:], ACT.Copy).then_inc(v_out, 1)
                    return
                if c == 2 * TT:
                    act.wait_ge(stack_ready, b.at(H, H))
                bank = O if j == 1 else Q
                act.activation(rows[:, par, t, j, :], bank[:], ACT.Copy)
                if c > 0 or b.first > 0 or j > 0:
                    act.wait_ge(ss_done, b.at(2 * TT, 2 * c + j))
                act.activation(squares[:], bank[:], ACT.Square, scale=SCALE).then_inc(raw_out, 1)

            def stack_out(b, h):
                act.wait_ge(stackT_done, b.at(H, h + 1))
                if h > 1 or b.first > 0:
                    act.wait_ge(scores_done, b.at(2 * H, 2 * h - 2))
                act.activation(stackT[0:SK, h % 2, :, :], TP[0:SK, :, :], ACT.Copy).then_inc(stackT_out, 1)

            def row(b, h):
                act.wait_ge(row_done, b.at(H, h + 1))
                act.activation(stackT[SK:SK + 1, h % 2, 0, :], TP[0:1, 0, :], ACT.Copy).then_inc(row_out, 1)

            def exponentials(b, h, half):
                act.wait_ge(scores_done, b.at(2 * H, 2 * h + half + 1))
                if half == 0:
                    before = h // HG - (2 if h % HG == 0 else 1)
                    if before >= 0 or b.first > 0:
                        act.wait_ge(pv_done, b.at(NG, before + 1))
                        act.wait_ge(sum_rows, b.at(H, HG * (before + 1)))
                act.activation(probs[:, buf(h), 2 * half:2 * half + 2, :], S[:], ACT.Exp, scale=SCALE
                               ).then_inc(exp_done, 1)

            def weighed_out(b, g):
                act.wait_ge(pv_done, b.at(NG, g + 1))
                if b.first > 1:
                    act.wait_ge(y_done, b.at(TT, -TT))
                act.activation(oT[:, b.parity, g, :], O[:], ACT.Copy).then_inc(o_out, 1)

            def copy_sums(b, g):
                act.wait_ge(sums_done, b.at(NG, g + 1))
                if g > 0 or b.first > 0:
                    act.wait_ge(o_ready, b.at(NG, g))
                act.activation(sums[:], TP[:, 1, :], ACT.Copy).then_inc(sums_out, 1)

            def stack_high(b, h):
                if h == 0:
                    act.wait_ge(rope_step, b.at(6 * TT, 6 * TT))
                if h > 0 or b.first > 0:
                    act.wait_ge(stackT_done, b.at(H, h))
                src = rows[:, b.parity, :, :, h * E:(h + 1) * E]
                act.activation(stack_at(0, SK), src, ACT.Copy).then_inc(stack_hi, 1)
                act.activation(stack_at(E, SK + E), src, ACT.Copy).then_inc(stack_hi, 1)

            def body(b, has_next):
                has_prev = b.first > 0
                prev, nxt = b.plus(-1), b.plus(1)
                for h in range(H):
                    t, kind = h // 4, h % 4
                    group = (b, t - 1) if t > 0 else (prev, NG - 1)
                    exponentials(b, h, 0)
                    exponentials(b, h, 1)
                    if h + 2 < H or has_next:
                        stack_out(*((b, h + 2) if h + 2 < H else (nxt, h + 2 - H)))
                    if h + 3 < H or has_next:
                        stack_high(*((b, h + 3) if h + 3 < H else (nxt, h + 3 - H)))
                    if h + 1 < H or has_next:
                        row(*((b, h + 1) if h + 1 < H else (nxt, 0)))
                    if kind == 0 and (t > 0 or has_prev):
                        weighed_out(*group)
                    if kind == 0 and has_next:
                        move_out(b, TT + t, 2)
                    if kind == 0 and (t > 0 or has_prev):
                        copy_sums(*group)
                    if kind in (1, 2) and has_next:
                        move_out(b, TT + 1 + t, kind - 1)
                    if kind == 3 and has_next:
                        modulate(b, TT + 2 + t)

            b0, last = Batch(0), Batch(NB - 1)
            act.wait_ge(mod_ready, 4)
            modulate(b0, 0)
            for c in range(TT + 1):
                for j in range(3 if c < TT else 2):
                    move_out(b0, c, j)
                    if j == 0:
                        modulate(b0, c + 1)
            for h in range(2):
                stack_high(b0, h)
                stack_out(b0, h)
            stack_high(b0, 2)
            row(b0, 0)
            body(b0, True)
            with act.Fori(0, (NB - 2) // 2) as i:
                body(Batch(1, i), True)
                body(Batch(2, i), True)
            body(last, False)
            weighed_out(last, NG - 1)
            copy_sums(last, NG - 1)

        @block.vector
        def _(dve):
            dve.sem_inc(y_gated, 1)
            dve.wait_ge(consts, 6)
            dve.tensor_copy(ident_r[:], ident[:]).then_inc(ident_ready, 1)
            dve.wait_ge(cond_exp, 1)
            dve.tensor_scalar(silu_sb, silu_sb, 1.0, None, ALU.add).then_inc(silu_step, 1)
            dve.wait_ge(silu_step, 1)
            dve.reciprocal(silu_sb, silu_sb).then_inc(silu_step, 1)
            dve.wait_ge(silu_step, 2)
            dve.tensor_tensor(silu_sb, silu_sb, cond_sb, ALU.mult).then_inc(silu_ready, 1)
            dve.wait_ge(siluT_done, 1)
            dve.tensor_copy(siluT, TP[:, 0, 0:DT * NB].rearrange("p (c b) -> p c b", c=DT)
                            ).then_inc(siluT_ready, 1)
            dve.wait_ge(ld_w, 16)
            w_qk = w_raw[:, :, 0:2 * D].rearrange("p c (h e) -> p c h e", e=E)
            dve.tensor_reduce(w_mean, w_qk, AX.X, ALU.add).then_inc(w_step, 1)
            dve.wait_ge(w_step, 1)
            dve.tensor_scalar(w_mean, w_mean, 1.0 / E, None, ALU.mult).then_inc(w_step, 1)
            dve.wait_ge(w_step, 2)
            dve.tensor_tensor(w_qk, w_qk, w_mean.unsqueeze(3).to_broadcast([P, DT, 2 * H, E]), ALU.subtract
                              ).then_inc(w_step, 1)
            dve.wait_ge(w_step, 3)
            dve.tensor_copy(wqkv_hi[:], w_raw).then_inc(w_step, 1)
            dve.wait_ge(w_step, 4)
            dve.tensor_tensor(wqkv_lo[:], w_raw, wqkv_hi[:].bitcast(F32), ALU.subtract).then_inc(w_ready, 1)
            dve.wait_ge(mod_done, 1)
            dve.tensor_copy(gate_sb, Q[0:NB, :]).then_inc(mod_ready, 1)
            ss = M[:, 0, 0:NB * 2 * DT].rearrange("p (m b) -> p b m", b=NB)
            dve.tensor_copy(ss_sb[:, :, 0:DT], ss[:, :, 0:DT]).then_inc(mod_ready, 1)
            dve.tensor_scalar(ss_sb[:, :, DT:2 * DT], ss[:, :, DT:2 * DT], 1.0, None, ALU.add
                              ).then_inc(mod_ready, 1)
            dve.wait_ge(mod_ready, 3)
            dve.tensor_copy(shift_scale[:], ss_sb[:, 0:2, :]).then_inc(mod_ready, 1)
            dve.wait_ge(ld_tables, 16 * 3)
            for j in range(2):
                w = norm_w[:, j, 0:R].rearrange("p (i two) -> p i two", two=2)
                dve.tensor_copy(rope_same[:, :, j, R:E], norm_w[:, j, R:E].unsqueeze(1).to_broadcast([P, TT, R]))
                for t in range(TT):
                    pos = pos_sb[:, t, :].rearrange("p (i c) -> p i c", c=2)
                    dve.tensor_tensor(rope_same[:, t, j, 0:R].rearrange("p (i two) -> p i two", two=2),
                                      pos[:, :, 0:1].to_broadcast([P, PAIRS, 2]), w, ALU.mult)
                    dve.tensor_tensor(rope_pair[:, t, j, :].rearrange("p (i two) -> p i two", two=2),
                                      pos[:, :, 1:2].to_broadcast([P, PAIRS, 2]), w[:, :, ::-1], ALU.mult
                                      ).then_inc(table_step, 1)
            dve.wait_ge(table_step, 2 * TT)
            even = rope_pair[:].rearrange("p t j (i two) -> p (t j i) two", two=2)[:, :, 0:1]
            dve.tensor_scalar(even, even, -1.0, None, ALU.mult).then_inc(tables_ready, 1)
            dve.memset(stats[:], 1.0).then_inc(x_stats, 1)
            dve.wait_ge(x_stats, 1)

            NEWTON = 13

            def x_statistics(b, c):
                dve.wait_ge(ld_x[c % 2], b.at(16 * TT // 2, 16 * (c // 2 + 1)))
                if c > 0 or b.first > 0:
                    dve.wait_ge(x_stats, b.at(2 * TT, 2 * c + 1))
                dve.bn_stats(bn[:], xin[:, c % 2, :]).then_inc(x_stats, 1)

            def wait_to_aggregate(b, c):
                dve.wait_ge(x_stats, b.at(2 * TT, 2 * c + 2))
                if c > 0 or b.first > 0:
                    dve.wait_ge(x_norm, b.at(TT, c))

            def aggregate_x():
                dve.bn_aggr(stats[:, 0:2], bn[:]).then_inc(x_stats, 1)

            def square_sums(b, c, j):
                dve.wait_ge(raw_out, b.at(2 * TT, 2 * c + j + 1))
                dve.wait_ge(newton_step, b.at(NEWTON * TT, NEWTON * (c + 2)))
                dve.tensor_reduce(stats[:, 2 + j * H:2 + (j + 1) * H],
                                  squares[:].rearrange("p (h e) -> p h e", e=E), AX.X, ALU.add
                                  ).then_inc(ss_done, 1)

            def inverse_roots(b, c, first=1, last=NEWTON):
                if first == 1:
                    dve.wait_ge(x_stats, b.at(2 * TT, 2 * c + 3))
                    if c > 0 or b.first > 0:
                        dve.wait_ge(x_norm, b.at(TT, c))
                    if c > 1 or b.first > 0:
                        dve.wait_ge(ss_done, b.at(2 * TT, 2 * (c - 1)))
                    if c > 2 or b.first > 0:
                        dve.wait_ge(qk_norm, b.at(TT, c - 2))
                for n in range(first, last + 1):
                    if n > 1:
                        dve.wait_ge(newton_step, b.at(NEWTON * TT, NEWTON * c + n - 1))
                    if n == 1:
                        ins = dve.tensor_scalar(rstd[:], stats[:, 1:], EPS, None, ALU.add)
                    elif n == 2:
                        ins = dve.tensor_scalar(newton[:].bitcast(I32), rstd[:].bitcast(I32), 1, None,
                                                ALU.logical_shift_right)
                    elif n == 3:
                        ins = dve.tensor_scalar(half_var[:], rstd[:], -0.5, None, ALU.mult)
                    elif n == 4:
                        ins = dve.tensor_scalar(rstd[:].bitcast(I32), newton[:].bitcast(I32), -1.0,
                                                float(RSQRT_MAGIC), ALU.mult, ALU.add)
                    elif n % 3 == 2:
                        ins = dve.tensor_tensor(newton[:], rstd[:], rstd[:], ALU.mult)
                    elif n % 3 == 0:
                        ins = dve.tensor_tensor(newton[:], newton[:], half_var[:], ALU.mult)
                    else:
                        ins = dve.scalar_tensor_tensor(rstd[:], newton[:], 1.5, rstd[:], ALU.add, ALU.mult)
                    ins.then_inc(newton_step, 1)

            def normalize_x(b, c):
                dve.wait_ge(newton_step, b.at(NEWTON * TT, NEWTON * (c + 1)))
                xt = xin[:, c % 2, :]
                dve.tensor_scalar(xt, xt, stats[:, 0:1], rstd[:, 0:1], ALU.subtract, ALU.mult
                                  ).then_inc(x_norm, 1)

            def normalize_qk(b, c):
                dve.wait_ge(newton_step, b.at(NEWTON * TT, NEWTON * (c + 3)))
                par = (b.first + c // TT) % 2
                qk = rows[:, par, c % TT, :, :].rearrange("p j (h e) -> p (j h) e", e=E)
                dve.tensor_tensor(qk, qk, rstd[:, 1:].unsqueeze(2).to_broadcast([P, 2 * H, E]), ALU.mult
                                  ).then_inc(qk_norm, 1)

            def x_parts(b, c):
                flat = "p c t -> p (c t)"
                dve.wait_ge(h_ready, b.at(TT, c + 1))
                if c > 0 or b.first > 0:
                    dve.wait_ge(proj_done, b.at(3 * TT, 3 * c))
                dve.tensor_copy(hT_hi[:].rearrange(flat), hT[:].rearrange(flat)).then_inc(h_hi, 1)
                dve.wait_ge(h_hi, b.at(TT, c + 1))
                dve.tensor_tensor(hT_lo[:].rearrange(flat), hT[:].rearrange(flat),
                                  hT_hi[:].rearrange(flat).bitcast(F32), ALU.subtract).then_inc(h_lo, 1)

            def stack_low(b, h):
                dve.wait_ge(stack_hi, b.at(2 * H, 2 * h + 2))
                src = rows[:, b.parity, :, :, h * E:(h + 1) * E]
                dve.tensor_tensor(stack_at(2 * E, SK - E), src, stack_at(0, SK).bitcast(F32), ALU.subtract
                                  ).then_inc(stack_ready, 1)

            def maximum(b, h, t):
                dve.wait_ge(max_scores, b.at(TT * H, TT * h + t + 1))
                if t == 0 and (h > 1 or b.first > 0):
                    dve.wait_ge(row_done, b.at(H, h - 1))
                dve.tensor_reduce(neg_max[:, h % 2, t:t + 1], M[:, t % 2, :], AX.X, ALU.max, negate=True
                                  ).then_inc(max_out, 1)

            def invert_sums(b, g, n):
                if n == 0:
                    dve.wait_ge(sums_out, b.at(NG, g + 1))
                part = sums[:, n * P:(n + 1) * P]
                dve.reciprocal(part, part).then_inc(recip_done, 1)

            def normalize_o(b, g):
                dve.wait_ge(recip_done, b.at(TT * NG, TT * (g + 1)))
                dve.wait_ge(o_out, b.at(NG, g + 1))
                o = oT[:, b.parity, g, :]
                dve.tensor_tensor(o, o, sums[:], ALU.mult).then_inc(o_ready, 1)

            def apply_gate(b, t):
                dve.wait_ge(y_done, b.at(TT, t + 1))
                if t == 0:
                    dve.wait_ge(ld_gate, b.at(16, 16))
                dve.wait_ge(y_ready, b.at(TT, t + 1))
                dve.tensor_tensor(gated[:], O[:], gate[:], ALU.mult).then_inc(y_gated, 1)

            def body(b, has_next):
                has_prev = b.first > 0
                prev, nxt = b.plus(-1), b.plus(1)
                for h in range(H):
                    t, kind = h // 4, h % 4
                    c = TT + 1 + t
                    group = (b, t - 1) if t > 0 else (prev, NG - 1)
                    grouped = t > 0 or has_prev
                    side = [[], [], [], []]
                    if has_next:
                        if kind == 0:
                            side[1].append((normalize_qk, (b, c - 1)))
                            side[2].append((x_parts, (b, c)))
                        if kind == 2:
                            side[2].append((square_sums, (b, c, 0)))
                            side[3].append((x_statistics, (b, c + 2)))
                        if kind == 3:
                            side[0] += [(wait_to_aggregate, (b, c + 2)), (square_sums, (b, c, 1)),
                                        (aggregate_x, ()), (inverse_roots, (b, c + 2, 1, 2))]
                            side[1].append((inverse_roots, (b, c + 2, 3, 6)))
                            side[2].append((inverse_roots, (b, c + 2, 7, NEWTON)))
                            side[3].append((normalize_x, (b, c + 2)))
                    if grouped and kind == 1:
                        for n, place in enumerate((1, 2, 3, 3)):
                            side[place].append((invert_sums, (*group, n)))
                    if grouped and kind == 2:
                        side[1].append((normalize_o, group))
                    if kind == 3 and has_prev:
                        side[3].append((apply_gate, (prev, t)))

                    def beside(n):
                        for step, args in side[n]:
                            step(*args)

                    beside(0)
                    for n in range(TT):
                        if h + 1 < H or has_next:
                            maximum(*((b, h + 1) if h + 1 < H else (nxt, 0)), n)
                        if n == 1:
                            beside(1)
                    beside(2)
                    if h + 3 < H or has_next:
                        stack_low(*((b, h + 3) if h + 3 < H else (nxt, h + 3 - H)))
                    beside(3)

            b0, last = Batch(0), Batch(NB - 1)
            for c in range(2):
                x_statistics(b0, c)
                wait_to_aggregate(b0, c)
                aggregate_x()
                inverse_roots(b0, c)
                normalize_x(b0, c)
            for c in range(TT + 1):
                x_parts(b0, c)
                x_statistics(b0, c + 2)
                square_sums(b0, c, 0)
                wait_to_aggregate(b0, c + 2)
                square_sums(b0, c, 1)
                aggregate_x()
                inverse_roots(b0, c + 2)
                normalize_x(b0, c + 2)
                if c < TT:
                    normalize_qk(b0, c)
            stack_low(b0, 0)
            stack_low(b0, 1)
            for t in range(TT):
                maximum(b0, 0, t)
            stack_low(b0, 2)
            body(b0, True)
            with dve.Fori(0, (NB - 2) // 2) as i:
                body(Batch(1, i), True)
                body(Batch(2, i), True)
            body(last, False)
            for n in range(TT):
                invert_sums(last, NG - 1, n)
            normalize_o(last, NG - 1)
            for t in range(TT):
                apply_gate(last, t)

        @block.gpsimd
        def _(pool):
            pool.sem_inc(y_ready, 1)
            pool.memset(ident[:], 0.0).then_inc(consts, 1)
            pool.wait_ge(consts, 1)
            pool.memset(ones[:], 1.0).then_inc(consts, 1)
            for n in range(2):
                pool.wait_ge(consts, 2 + n)
                pool.memset(stackT[SK:SK + 1, n, 1, :].bitcast(F32), 1.0).then_inc(consts, 1)
            pool.wait_ge(consts, 4)
            pool.affine_select(out=ident[:], in_=ident[:], compare_op=ALU.not_equal, fill=1.0, base=0,
                               pattern=[[-1, P]], channel_multiplier=1).then_inc(consts, 2)

            def rotate(b, c, js=(0, 1)):
                pool.wait_ge(qk_norm, b.at(TT, c + 1))
                par, t = (b.first + c // TT) % 2, c % TT
                for j in js:
                    n = 6 * c + 3 * j
                    r = rows[:, par, t, j, :].rearrange("p (h e) -> p h e", e=E)
                    swapped = bass.AP(tensor=r.tensor, offset=r.offset + 1,
                                      ap=[r.ap[0], [E, H], [2, PAIRS], [-1, 2]])
                    if n > 0 or b.first > 0:
                        pool.wait_ge(rope_step, b.at(6 * TT, n))
                    pool.tensor_tensor(pair_part[:].rearrange("p h (i two) -> p h i two", two=2), swapped,
                                       rope_pair[:, t, j, :].rearrange("p (i two) -> p i two", two=2)
                                       .unsqueeze(1).to_broadcast([P, H, PAIRS, 2]), ALU.mult
                                       ).then_inc(rope_step, 1)
                    pool.wait_ge(rope_step, b.at(6 * TT, n + 1))
                    pool.tensor_tensor(r, r, rope_same[:, t, j, :].unsqueeze(1).to_broadcast([P, H, E]),
                                       ALU.mult).then_inc(rope_step, 1)
                    pool.wait_ge(rope_step, b.at(6 * TT, n + 2))
                    last = pool.tensor_tensor(r[:, :, 0:R], r[:, :, 0:R], pair_part[:], ALU.add)
                    last.then_inc(rope_step, 1)

            def sum_key_tiles(b, h):
                n = buf(h)
                before = h // HG - (2 if h % HG == 0 else 1)
                pool.wait_ge(exp_done, b.at(2 * H, 2 * h + 1))
                if before >= 0 or b.first > 0:
                    pool.wait_ge(sums_done, b.at(NG, before + 1))
                pool.tensor_tensor(colsum[:, n, :], probs[:, n, 0, :], probs[:, n, 1, :], ALU.add
                                   ).then_inc(sum_step, 1)
                pool.wait_ge(sum_step, b.at(2 * H, 2 * h + 1))
                pool.wait_ge(exp_done, b.at(2 * H, 2 * h + 2))
                pool.tensor_tensor(colsum[:, n, :], colsum[:, n, :], probs[:, n, 2, :], ALU.add
                                   ).then_inc(sum_step, 1)
                pool.wait_ge(sum_step, b.at(2 * H, 2 * h + 2))
                pool.tensor_tensor(colsum[:, n, :], colsum[:, n, :], probs[:, n, 3, :], ALU.add
                                   ).then_inc(sum_rows, 1)

            def add_residual(b, t):
                pool.wait_ge(y_gated, b.at(TT, t + 2))
                pool.wait_ge(ld_res[t % 2], b.at(32, 16 * (t // 2 + 1)))
                r = xres[:, t % 2, :]
                pool.tensor_tensor(r, r, gated[:], ALU.add).then_inc(y_ready, 1)

            def body(b, has_next):
                prev = b.plus(-1)
                for h in range(H):
                    t, kind = h // 4, h % 4
                    if kind == 0 and has_next:
                        rotate(b, TT + t)
                    sum_key_tiles(b, h)
                    if kind == 3 and b.first > 0:
                        add_residual(prev, t)

            b0, last = Batch(0), Batch(NB - 1)
            pool.wait_ge(tables_ready, 1)
            for t in range(TT):
                rotate(b0, t)
            body(b0, True)
            with pool.Fori(0, (NB - 2) // 2) as i:
                body(Batch(1, i), True)
                body(Batch(2, i), True)
            body(last, False)
            for t in range(TT):
                add_residual(last, t)


_INS = ["x", "cond_1024", "L0_cond_position", "L0_cond_mod_w", "L0_cond_mod_b", "L0_cond_w_qkv",
        "L0_cond_w_out", "L0_cond_q_norm_w", "L0_cond_k_norm_w"]


def kernel(**inputs):
    import numpy as _np
    import concourse.bacc as _bacc
    from concourse import mybir as _mybir
    from concourse.bass_utils import run_bass_kernel_spmd as _run

    nc = _bacc.Bacc("TRN2", target_bir_lowering=False, num_devices=1)
    arrays, args = {}, []
    for name in _INS:
        a = _np.ascontiguousarray(inputs[name])
        arrays[f"in_{name}_dram"] = a
        args.append(nc.dram_tensor(f"in_{name}_dram", a.shape, _mybir.dt.from_np(a.dtype),
                                   kind="ExternalInput").ap())
    shape = tuple(inputs["x"].shape)
    args.append(nc.dram_tensor("out_0_dram", shape, _mybir.dt.float32, kind="ExternalOutput").ap())
    cond_attention_kernel(nc, *args)
    r = _run(nc, [arrays], core_ids=[0])
    return r.results[0]["out_0_dram"]
```

```python
from contextlib import ExitStack

import concourse.bass as bass
from concourse import mybir

ALU = mybir.AluOpType
ACT = mybir.ActivationFunctionType
AX = mybir.AxisListType
F32 = mybir.dt.float32
F32R = mybir.dt.float32r
I32 = mybir.dt.int32

P = 128
PROBS_BUF = ([3, 0, 1, 2], [4, 0, 1, 2])
FILL_PV, FILL_Q, FILL_K, FILL_V, FILL_OUT = (0, 1, 1, 2), (0, 0, 1, 1), (2, 2, 3, 3), (1, 1, 2, 2), (0, 1, 1, 2)
FILL_LAST_OUT = (1, 2, 0, 1)
RSQRT_MAGIC = 0x5F3759DF


class Batch:

    def __init__(self, first, i=None):
        self.first, self.i, self.parity = first, i, first % 2

    def at(self, per, more=0):
        known = per * self.first + more
        return known if self.i is None else self.i * (2 * per) + known

    def plus(self, n):
        return Batch(self.first + n, self.i)

    def wrapped(self, n):
        return self.first % n if self.i is None else (self.i * 2 + self.first) % n


def cond_attention_kernel(nc, x, cond, position, mod_w, mod_b, w_qkv, w_out, q_norm_w, k_norm_w, out):
    NB, T, D = x.shape
    E = q_norm_w.shape[0]
    H = D // E
    TT = T // P
    DT = D // P
    HG = P // E
    NG = H // HG
    R = E // 2
    PAIRS = R // 2
    SK = 3 * E
    EPS = 1e-6
    SCALE = float(E) ** -0.5
    assert TT == 4 and DT == 4 and HG == 4 and NG == 4 and NB % 2 == 0

    gate_rows = nc.dram_tensor("gate_rows", (NB, D), F32, kind="Internal").ap()
    mod_cols = nc.dram_tensor("mod_cols", (NB, P, 2 * DT), F32, kind="Internal").ap()
    x_t = x.rearrange("b (t p) d -> b t p d", p=P)
    out_t = out.rearrange("b (t p) d -> b t p d", p=P)

    with ExitStack() as ctx:
        def sb(name, shape, dt=F32):
            return ctx.enter_context(nc.sbuf_tensor(name, shape, dt))

        def sem(name):
            return ctx.enter_context(nc.semaphore(name))

        wqkv_hi = sb("wqkv_hi", [P, DT, 3 * D], F32R)
        wqkv_lo = sb("wqkv_lo", [P, DT, 3 * D], F32R)
        wout = sb("wout", [P, DT, D])
        ident = sb("ident", [P, P])
        ident_r = sb("ident_r", [P, P], F32R)
        ones = sb("ones", [P, E])
        rope_same = sb("rope_same", [P, TT, 2, E])
        rope_pair = sb("rope_pair", [P, TT, 2, R])
        shift_scale = sb("shift_scale", [P, 2, 2 * DT])
        gate = sb("gate", [P, D])
        xin = sb("xin", [P, 2, D])
        hT = sb("hT", [P, DT, P])
        hT_hi = sb("hT_hi", [P, DT, P], F32R)
        hT_lo = sb("hT_lo", [P, DT, P], F32R)
        squares = sb("squares", [P, D])
        rows = sb("rows", [P, 2, TT, 2, D])
        pair_part = sb("pair_part", [P, H, R])
        vals = sb("vals", [P, 2, TT, D])
        stack = sb("stack", [P, TT, 2, SK], F32R)
        stackT = sb("stackT", [P, 2, 2, T], F32R)
        neg_max = sb("neg_max", [P, 2, TT], F32R)
        probs = sb("probs", [P, 5, TT, T])
        colsum = sb("colsum", [P, 5, T])
        oT = sb("oT", [P, 2, NG, T])
        xres = sb("xres", [P, 2, D])
        gated = sb("gated", [P, D])
        sums = sb("sums", [P, T])
        bn = sb("bn", [P, 6])
        stats = sb("stats", [P, 2 + 2 * H])
        half_var = sb("half_var", [P, 1 + 2 * H])
        rstd = sb("rstd", [P, 1 + 2 * H])
        newton = sb("newton", [P, 1 + 2 * H])

        S = ctx.enter_context(nc.psum_tensor("S", [P, 2, 512], F32))
        M = ctx.enter_context(nc.psum_tensor("M", [P, 2, 512], F32))
        TP = ctx.enter_context(nc.psum_tensor("TP", [P, 2, 512], F32))
        Q = ctx.enter_context(nc.psum_tensor("Q", [P, 512], F32))
        O = ctx.enter_context(nc.psum_tensor("O", [P, 512], F32))

        ld_modw, ld_modb, ld_wout = sem("ld_modw"), sem("ld_modb"), sem("ld_wout")
        ld_w = [sem("ld_wq"), sem("ld_wk"), sem("ld_wv")]
        ld_cond, ld_tables = sem("ld_cond"), sem("ld_tables")
        ld_x = [sem("ld_x0"), sem("ld_x1")]
        ld_res = [sem("ld_res0"), sem("ld_res1")]
        st_y = [sem("st_y0"), sem("st_y1")]
        ld_ss, ld_gate, ld_last, st_mod = sem("ld_ss"), sem("ld_gate"), sem("ld_last"), sem("st_mod")
        xT_done, proj_done, stackT_done, max_scores, row_done = (
            sem("xT_done"), sem("proj_done"), sem("stackT_done"), sem("max_scores"), sem("row_done"))
        scores_done, pv_done, sums_done, y_done, siluT_done, ss_product, gate_product = (
            sem("scores_done"), sem("pv_done"), sem("sums_done"), sem("y_done"), sem("siluT_done"),
            sem("ss_product"), sem("gate_product"))
        stackT_out, row_out, exp_done, h_ready, raw_out, v_out, o_out, sums_out, cond_exp = (
            sem("stackT_out"), sem("row_out"), sem("exp_done"), sem("h_ready"), sem("raw_out"), sem("v_out"),
            sem("o_out"), sem("sums_out"), sem("cond_exp"))
        squared, w_high, gate_ready = sem("squared"), sem("w_high"), sem("gate_ready")
        max_out, stack_hi, stack_ready, x_stats, x_norm, h_hi, h_lo = (
            sem("max_out"), sem("stack_hi"), sem("stack_ready"), sem("x_stats"), sem("x_norm"), sem("h_hi"),
            sem("h_lo"))
        ss_done, newton_step, qk_norm, recip_done, o_ready, y_gated = (
            sem("ss_done"), sem("newton_step"), sem("qk_norm"), sem("recip_done"), sem("o_ready"),
            sem("y_gated"))
        ident_ready, silu_ready, siluT_ready, ss_ready, w_low, tables_ready = (
            sem("ident_ready"), sem("silu_ready"), sem("siluT_ready"), sem("ss_ready"), sem("w_low"),
            sem("tables_ready"))
        silu_step, modb_ready, w_step, w_centred, table_step = (
            sem("silu_step"), sem("modb_ready"), sem("w_step"), sem("w_centred"), sem("table_step"))
        rope_step, sum_step, sum_rows, y_ready, consts = (
            sem("rope_step"), sem("sum_step"), sem("sum_rows"), sem("y_ready"), sem("consts"))

        w_raw = probs[:, 0:3].rearrange("p a t q -> p (a t q)").rearrange("p (c n) -> p c n", c=DT)
        modw_raw = rows[:].rearrange("p a t j d -> p (a t j d)")[:, 0:DT * 3 * D].rearrange(
            "p (c n) -> p c n", c=DT)
        cond_sb = oT[0:NB, 0, 0, :]
        silu_sb = oT[0:NB, 0, 1, :]
        siluT = oT[:, 0, 2, 0:DT * NB].rearrange("p (c b) -> p c b", c=DT)
        modb_row = oT[0:1, 1, 0, :]
        modb_rows = oT[0:2 * DT, 1, 1, 0:P]
        modb_cols = oT[:, 1, 2, 0:2 * DT]
        gate_sb = probs[0:NB, 3, 0, :]
        ss_sb = oT[:, 0, 3, 0:NB * 2 * DT].rearrange("p (b m) -> p b m", b=NB)
        w_mean = colsum[:, 0, 0:DT * 2 * H].rearrange("p (j c h) -> p j c h", j=2, c=DT)
        pos_sb = xres[:, 0, 0:TT * R].rearrange("p (t c) -> p t c", t=TT)
        norm_w = xres[:, 1, 0:2 * E].rearrange("p (j e) -> p j e", j=2)

        def buf(h):
            return PROBS_BUF[(h // HG) % 2][h % HG]

        def stack_at(offset, j_step):
            whole = stack[:]
            return bass.AP(tensor=whole.tensor, offset=whole.offset + offset,
                           ap=[whole.ap[0], [2 * SK, TT], [j_step, 2], [1, E]])

        last_res = [xin[:, 0, :], xin[:, 1, :], xres[:, 0, :], xres[:, 1, :]]
        last_banks = [S[:, 0, :], S[:, 1, :], M[:, 0, :], M[:, 1, :]]

        parts_alt = [stackT[:, n, 0, :].rearrange("p (c t) -> p c t", c=DT) for n in range(2)]

        def x_buffers(b, c):
            if b.i is None and b.first == 0 and c < TT and c % 2 == 1:
                return parts_alt[0], parts_alt[1]
            return hT_hi[:], hT_lo[:]

        block = ctx.enter_context(nc.Block())

        @block.sync
        def _(sp):
            sp.dma_start(cond_sb, cond).then_inc(ld_cond, 16)
            sp.dma_start(modb_rows, mod_b[0:2 * D].rearrange("(m p) -> m p", p=P)).then_inc(ld_cond, 16)
            sp.dma_start(modw_raw, mod_w.rearrange("(c p) n -> p c n", p=P)).then_inc(ld_modw, 16)
            sp.dma_start(pos_sb, position.rearrange("(t p) i c -> p t (i c)", p=P)).then_inc(ld_tables, 16)
            for j, w in enumerate((q_norm_w, k_norm_w)):
                sp.dma_start(norm_w[:, j, :], w.rearrange("(a e) -> a e", a=1).to_broadcast([P, E])
                             ).then_inc(ld_tables, 16)
            for t in range(2):
                sp.dma_start(xin[:, t, :], x_t[0, t]).then_inc(ld_x[t], 16)
            sp.dma_start(modb_row, mod_b[2 * D:3 * D].rearrange("(a n) -> a n", a=1)).then_inc(ld_modb, 16)
            for j in range(3):
                cols = slice(j * D, (j + 1) * D)
                sp.dma_start(w_raw[:, :, cols], w_qkv[:, cols].rearrange("(c p) n -> p c n", p=P)
                             ).then_inc(ld_w[j], 16)
            sp.dma_start(wout[:], w_out.rearrange("(c p) n -> p c n", p=P)).then_inc(ld_wout, 16)

            def load_x(batch, tile, c, b):
                sp.wait_ge(xT_done, b.at(TT, c - 1))
                sp.dma_start(xin[:, c % 2, :], x_t[bass.ds(batch, 1), tile].rearrange("b p d -> (b p) d")
                             ).then_inc(ld_x[c % 2], 16)

            b0 = Batch(0)
            for t in range(2, TT):
                load_x(0, t, t, b0)
            for t in range(2):
                load_x(1, t, TT + t, b0)
            load_x(1, 2, TT + 2, b0)
            sp.wait_ge(ss_ready, 4)
            sp.wait_ge(gate_ready, 1)
            sp.dma_start(gate_rows, gate_sb).then_inc(st_mod, 16)
            sp.dma_start(mod_cols.rearrange("b p m -> p b m"), ss_sb).then_inc(st_mod, 16)
            sp.wait_ge(st_mod, 32)

            def store_and_load(b, more):
                prev = b.plus(-1)
                if more:
                    sp.wait_ge(h_ready, b.at(TT, TT))
                    sp.dma_start(shift_scale[:, b.parity, :],
                                 mod_cols[bass.ds(b.plus(2).wrapped(NB), 1)].rearrange("b p m -> (b p) m")
                                 ).then_inc(ld_ss, 16)
                if b.first > 0:
                    sp.wait_ge(y_gated, prev.at(TT, 1))
                    sp.dma_start(gate[:], gate_rows[bass.ds(prev.at(1), 1)].to_broadcast([P, D])
                                 ).then_inc(ld_gate, 16)
                for t in range(TT):
                    if b.first > 0:
                        if b.first == 1 and t == 0:
                            sp.wait_ge(tables_ready, 1)
                        if prev.first > 0 or t >= 2:
                            sp.wait_ge(st_y[t % 2], prev.at(2 * 16, 16 * (t // 2)))
                        sp.dma_start(xres[:, t % 2, :], x_t[bass.ds(prev.at(1), 1), t].rearrange(
                            "b p d -> (b p) d")).then_inc(ld_res[t % 2], 16)
                    if more:
                        batch = b.at(1, 1) if t == 0 else b.plus(2).wrapped(NB)
                        load_x(batch, (3 + t) % TT, TT + 3 + t, b)
                    if b.first > 0:
                        sp.wait_ge(y_ready, prev.at(TT, t + 2))
                        sp.dma_start(out_t[bass.ds(prev.at(1), 1), t].rearrange("b p d -> (b p) d"),
                                     xres[:, t % 2, :]).then_inc(st_y[t % 2], 16)

            store_and_load(Batch(0), True)
            with sp.Fori(0, (NB - 2) // 2) as i:
                store_and_load(Batch(1, i), True)
                store_and_load(Batch(2, i), True)
            sp.wait_ge(x_norm, NB * TT + 3)
            sp.wait_ge(xT_done, NB * TT + 2)
            for t in range(2):
                sp.dma_start(last_res[t], x_t[NB - 1, t]).then_inc(ld_last, 16)
            store_and_load(Batch(NB - 1), False)
            last = Batch(NB - 1)
            sp.wait_ge(y_gated, last.at(TT, 1))
            sp.dma_start(gate[:], gate_rows[NB - 1:NB].to_broadcast([P, D])).then_inc(ld_gate, 16)
            for t in (2, 3):
                sp.wait_ge(st_y[t % 2], last.at(2 * 16))
                sp.dma_start(last_res[t], x_t[NB - 1, t]).then_inc(ld_res[t % 2], 16)
            for t in range(TT):
                sp.wait_ge(y_ready, last.at(TT, t + 2))
                sp.dma_start(out_t[NB - 1, t], last_res[t]).then_inc(st_y[t % 2], 16)
            for t in range(2):
                sp.wait_ge(st_y[t], 2 * 16 * NB)

        @block.tensor
        def _(pe):
            def transpose_x(b, c):
                pe.wait_ge(x_norm, b.at(TT, c + 1))
                for k in range(DT):
                    mm = pe.transpose(TP[:, 1, k * P:(k + 1) * P], xin[:, c % 2, k * P:(k + 1) * P], ident[:])
                mm.then_inc(xT_done, 1)

            pe.wait_ge(consts, 6)
            pe.wait_ge(silu_ready, 1)
            for c in range(DT):
                pe.transpose(TP[:, 0, c * NB:(c + 1) * NB], silu_sb[:, c * P:(c + 1) * P], ident[0:NB, 0:NB])
            pe.transpose(TP[:, 0, DT * NB:DT * NB + 2 * DT], modb_rows, ident[0:2 * DT, 0:2 * DT]
                         ).then_inc(siluT_done, 1)
            pe.wait_ge(siluT_ready, 1)
            pe.wait_ge(ld_modw, 16)
            for m in range(2 * DT):
                for c in range(DT):
                    mm = pe.matmul(M[:, 0, m * NB:(m + 1) * NB], modw_raw[:, c, m * P:(m + 1) * P], siluT[:, c, :],
                                   start=(c == 0), stop=(c == DT - 1))
            mm.then_inc(ss_product, 1)
            pe.wait_ge(ident_ready, 1)
            transpose_x(Batch(0), 0)
            pe.wait_ge(ld_modb, 16)
            cols = slice(2 * D, 3 * D)
            for c in range(DT):
                pe.matmul(M[0:NB, 1, :], siluT[:, c, :], modw_raw[:, c, cols], start=(c == 0), stop=False)
            pe.matmul(M[0:NB, 1, :], ones[0:1, 0:NB], modb_row, start=False, stop=True).then_inc(gate_product, 1)

            def project(b, c, j, n):
                if n == 0 and j == 0:
                    pe.wait_ge(h_lo, b.at(TT, c + 1))
                    if c > 0 or b.first > 0:
                        pe.wait_ge(v_out, b.at(TT, c))
                if n == 0 and j == 1:
                    if c > 0 or b.first > 0:
                        pe.wait_ge(raw_out, b.at(2 * TT, 2 * c))
                    if c > TT + 1 or b.first > 0:
                        pe.wait_ge(o_out, b.at(NG, c - TT - 1))
                if n == 0 and j == 2:
                    pe.wait_ge(raw_out, b.at(2 * TT, 2 * c + 1))
                x_hi, x_lo = x_buffers(b, c)
                terms = [(a, w, k) for k in range(DT)
                         for a, w in ((x_hi, wqkv_hi), (x_hi, wqkv_lo), (x_lo, wqkv_hi))]
                bank = O if j == 1 else Q
                for m in range(3 * n, 3 * n + 3):
                    a, w, k = terms[m]
                    mm = pe.matmul(bank[:], a[:, k, :], w[:, k, j * D:(j + 1) * D], start=(m == 0), stop=(m == 11))
                if n == 3:
                    mm.then_inc(proj_done, 1)

            def stack_transposes(b, h):
                pe.wait_ge(stack_ready, b.at(H, h + 1))
                if h > 1 or b.first > 0:
                    pe.wait_ge(row_out, b.at(H, h - 1))
                for j in range(2):
                    for t in range(TT):
                        mm = pe.transpose(TP[0:SK, j, t * P:(t + 1) * P].bitcast(F32R), stack[:, t, j, :],
                                          ident_r[:])
                mm.then_inc(stackT_done, 1)

            def scores_for_max(b, h, t):
                if t == 0:
                    pe.wait_ge(stackT_out, b.at(H, h + 1))
                if h > 0 or b.first > 0 or t >= 2:
                    pe.wait_ge(max_out, b.at(TT * H, TT * h + t - 1))
                qT, kT = stackT[0:SK, h % 2, 0, :], stackT[0:SK, h % 2, 1, :]
                pe.matmul(M[:, t % 2, :], qT[:, t * P:(t + 1) * P], kT, start=True, stop=True
                          ).then_inc(max_scores, 1)

            def max_row(b, h, stacks):
                pe.wait_ge(max_out, b.at(TT * H, TT * (h + 1)))
                pe.wait_ge(stackT_out, b.at(H, stacks))
                for t in range(TT):
                    mm = pe.transpose(TP[0:1, 0, t * P:(t + 1) * P].bitcast(F32R), neg_max[:, h % 2, t:t + 1],
                                      ident_r[:])
                mm.then_inc(row_done, 1)

            def scores(b, h, half):
                if half == 0:
                    pe.wait_ge(row_out, b.at(H, h + 1))
                if h > 0 or b.first > 0 or half:
                    pe.wait_ge(exp_done, b.at(2 * H, 2 * h + half))
                qT, kT = stackT[0:SK + 1, h % 2, 0, :], stackT[0:SK + 1, h % 2, 1, :]
                for t in range(2):
                    k = 2 * half + t
                    mm = pe.matmul(S[:, t, :], kT[:, k * P:(k + 1) * P], qT, start=True, stop=True)
                mm.then_inc(scores_done, 1)

            def weigh_values(b, g, k, has_next=True):
                if k == 0:
                    pe.wait_ge(exp_done, b.at(2 * H, 2 * HG * (g + 1)))
                    pe.wait_ge(v_out, b.at(TT, TT))
                    if has_next:
                        pe.wait_ge(raw_out, b.at(2 * TT, 2 * (TT + 1 + g) + 2))
                    if b.first > 0 or g == NG - 1:
                        pe.wait_ge(y_gated, b.at(TT, g - TT + 2))
                for i in range(HG):
                    h = HG * g + i
                    mm = pe.matmul(O[E * i:E * (i + 1), :], vals[:, b.parity, k, E * h:E * (h + 1)],
                                   probs[:, buf(h), k, :], start=(k == 0), stop=(k == TT - 1),
                                   skip_group_check=True)
                if k == TT - 1:
                    mm.then_inc(pv_done, 1)

            def column_sums(b, g):
                pe.wait_ge(sum_rows, b.at(H, HG * (g + 1)))
                for i in range(HG):
                    mm = pe.matmul(TP[E * i:E * (i + 1), 1, :], ones[:, 0:E], colsum[:, buf(HG * g + i), :],
                                   start=True, stop=True, skip_group_check=True)
                mm.then_inc(sums_done, 1)

            def project_out(b, t, g, last):
                bank = Q if last else O
                if g == 0:
                    pe.wait_ge(o_ready, b.at(NG, NG))
                    if not last:
                        pe.wait_ge(raw_out, b.at(2 * TT, 2 * (2 * TT + 1 + t) + 2))
                    elif t == 0:
                        pe.wait_ge(v_out, b.at(TT, 2 * TT))
                    else:
                        pe.wait_ge(y_gated, b.at(TT, t + 1))
                mm = pe.matmul(bank[:], oT[:, b.parity, g, t * P:(t + 1) * P], wout[:, g, :],
                               start=(g == 0), stop=(g == NG - 1))
                if g == NG - 1:
                    mm.then_inc(y_done, 1)

            def project_last(g, t):
                if g == 0 and t == 2:
                    pe.wait_ge(max_out, NB * TT * H)
                mm = pe.matmul(last_banks[t], oT[:, 1, g, t * P:(t + 1) * P], wout[:, g, :],
                               start=(g == 0), stop=(g == NG - 1))
                if g == NG - 1:
                    mm.then_inc(y_done, 1)

            def body(b, has_next):
                has_prev = b.first > 0
                prev, nxt = b.plus(-1), b.plus(1)
                for h in range(H):
                    t, kind = h // 4, h % 4
                    c = TT + 1 + t
                    group = (b, t - 1) if t > 0 else (prev, NG - 1)
                    grouped = t > 0 or has_prev
                    one, two = h + 1 < H or has_next, h + 2 < H or has_next
                    head1 = (b, h + 1) if h + 1 < H else (nxt, 0)
                    head2 = (b, h + 2) if h + 2 < H else (nxt, h + 2 - H)

                    def lay(place):
                        if kind == 0 and grouped:
                            for k in range(TT):
                                if FILL_PV[k] == place:
                                    weigh_values(*group, k, has_next or t == 0)
                            if place == 2:
                                column_sums(*group)
                        if kind == 1 and has_next:
                            for j, places in enumerate((FILL_Q, FILL_K)):
                                for n in range(4):
                                    if places[n] == place:
                                        project(b, c, j, n)
                        if kind == 2 and has_next:
                            for n in range(4):
                                if FILL_K[n] == place + 3:
                                    project(b, c, 1, n)
                            for n in range(4):
                                if FILL_V[n] == place:
                                    project(b, c, 2, n)
                        if kind == 3 and has_next and place == 2:
                            transpose_x(b, c + 1)
                        if kind == 3 and has_next and has_prev:
                            for g in range(NG):
                                if FILL_OUT[g] == place:
                                    project_out(prev, t, g, False)
                        if kind >= 2 and not has_next:
                            for g in range(2 * kind - 4, 2 * kind - 2):
                                if FILL_LAST_OUT[g] == place:
                                    project_out(prev, t, g, True)
                        if h == H - 1 and not has_next and place == 2:
                            project_last(0, 2)
                            project_last(0, 3)

                    scores(b, h, 0)
                    if one:
                        scores_for_max(*head1, 0)
                        scores_for_max(*head1, 1)
                    lay(0)
                    scores(b, h, 1)
                    if two:
                        if kind == 0 and (has_next or t == 0):
                            pe.wait_ge(h_ready, b.at(TT, c + 1))
                        if kind == 1 and grouped:
                            pe.wait_ge(sums_out, group[0].at(NG, group[1] + 1))
                        stack_transposes(*head2)
                    if one:
                        scores_for_max(*head1, 2)
                        scores_for_max(*head1, 3)
                    lay(1)
                    if one:
                        max_row(*head1, head1[1] + (2 if two else 1))
                    lay(2)

            b0, last = Batch(0), Batch(NB - 1)
            for c in range(TT + 1):
                for j in range(3):
                    if c == 0:
                        pe.wait_ge(w_low, j + 1)
                    if c == 1 and j == 0:
                        pe.wait_ge(gate_ready, 1)
                    for n in range(4):
                        project(b0, c, j, n)
                    if j == 0:
                        pe.wait_ge(h_ready, c + 1)
                        transpose_x(b0, c + 1)
            pe.wait_ge(h_ready, TT + 2)
            pe.wait_ge(ld_wout, 16)
            stack_transposes(b0, 0)
            pe.wait_ge(stackT_out, 1)
            stack_transposes(b0, 1)
            for t in range(TT):
                scores_for_max(b0, 0, t)
            max_row(b0, 0, 2)
            body(b0, True)
            with pe.Fori(0, (NB - 2) // 2) as i:
                body(Batch(1, i), True)
                body(Batch(2, i), True)
            body(last, False)
            for k in range(TT):
                weigh_values(last, NG - 1, k, False)
            column_sums(last, NG - 1)
            pe.wait_ge(exp_done, last.at(2 * H, 2 * H))
            pe.wait_ge(o_ready, last.at(NG, NG - 1))
            for g in range(NG):
                if g == NG - 1:
                    pe.wait_ge(o_ready, last.at(NG, NG))
                for t in range(TT):
                    if g > 0 or t < 2:
                        project_last(g, t)

        @block.scalar
        def _(act):
            act.wait_ge(ld_cond, 32)
            act.activation(silu_sb, cond_sb, ACT.Exp, scale=-1.0).then_inc(cond_exp, 1)

            def weight_high(j):
                cols = slice(j * D, (j + 1) * D)
                act.activation(wqkv_hi[:, :, cols], w_raw[:, :, cols], ACT.Copy).then_inc(w_high, 1)

            def modulate(b, c):
                par = (b.first + c // TT) % 2
                if c == 2 * TT:
                    act.wait_ge(ld_ss, b.at(16, 16))
                act.wait_ge(xT_done, b.at(TT, c + 1))
                if c > 0 or b.first > 0:
                    act.wait_ge(h_lo, b.at(TT, c))
                for k in range(DT):
                    last = act.activation(hT[:, k, :], TP[:, 1, k * P:(k + 1) * P], ACT.Identity,
                                          bias=shift_scale[:, par, k:k + 1],
                                          scale=shift_scale[:, par, DT + k:DT + k + 1])
                last.then_inc(h_ready, 1)

            def move_out(b, c, j):
                act.wait_ge(proj_done, b.at(3 * TT, 3 * c + j + 1))
                par, t = (b.first + c // TT) % 2, c % TT
                if j == 2:
                    if t == 0 and b.first > 0:
                        act.wait_ge(pv_done, b.at(NG, 0))
                    act.activation(vals[:, par, t, :], Q[:], ACT.Copy).then_inc(v_out, 1)
                    return
                if c == 2 * TT:
                    act.wait_ge(stack_ready, b.at(H, H))
                bank = O if j == 1 else Q
                if c > 0 or b.first > 0 or j > 0:
                    act.wait_ge(ss_done, b.at(2 * TT, 2 * c + j))
                act.activation(squares[:], bank[:], ACT.Square, scale=SCALE).then_inc(squared, 1)
                act.activation(rows[:, par, t, j, :], bank[:], ACT.Copy).then_inc(raw_out, 1)

            def stack_out(b, h):
                act.wait_ge(stackT_done, b.at(H, h + 1))
                if h > 1 or b.first > 0:
                    act.wait_ge(scores_done, b.at(2 * H, 2 * h - 2))
                act.activation(stackT[0:SK, h % 2, :, :], TP[0:SK, :, :], ACT.Copy).then_inc(stackT_out, 1)

            def row(b, h):
                act.wait_ge(row_done, b.at(H, h + 1))
                act.activation(stackT[SK:SK + 1, h % 2, 0, :], TP[0:1, 0, :], ACT.Copy).then_inc(row_out, 1)

            def exponentials(b, h, half):
                act.wait_ge(scores_done, b.at(2 * H, 2 * h + half + 1))
                if half == 0:
                    before = h // HG - (2 if h % HG == 0 else 1)
                    if before >= 0 or b.first > 0:
                        act.wait_ge(pv_done, b.at(NG, before + 1))
                        act.wait_ge(sum_rows, b.at(H, HG * (before + 1)))
                act.activation(probs[:, buf(h), 2 * half:2 * half + 2, :], S[:], ACT.Exp, scale=SCALE
                               ).then_inc(exp_done, 1)

            def weighed_out(b, g):
                act.wait_ge(pv_done, b.at(NG, g + 1))
                if b.first > 1:
                    act.wait_ge(y_done, b.at(TT, -TT))
                act.activation(oT[:, b.parity, g, :], O[:], ACT.Copy).then_inc(o_out, 1)

            def copy_sums(b, g):
                act.wait_ge(sums_done, b.at(NG, g + 1))
                if g > 0 or b.first > 0:
                    act.wait_ge(o_ready, b.at(NG, g))
                act.activation(sums[:], TP[:, 1, :], ACT.Copy).then_inc(sums_out, 1)

            def stack_high(b, h):
                if h == 0:
                    act.wait_ge(rope_step, b.at(6 * TT, 6 * TT))
                if h > 0 or b.first > 0:
                    act.wait_ge(stackT_done, b.at(H, h))
                src = rows[:, b.parity, :, :, h * E:(h + 1) * E]
                act.activation(stack_at(0, SK), src, ACT.Copy).then_inc(stack_hi, 1)
                act.activation(stack_at(E, SK + E), src, ACT.Copy).then_inc(stack_hi, 1)

            def body(b, has_next):
                has_prev = b.first > 0
                prev, nxt = b.plus(-1), b.plus(1)
                for h in range(H):
                    t, kind = h // 4, h % 4
                    group = (b, t - 1) if t > 0 else (prev, NG - 1)
                    exponentials(b, h, 0)
                    exponentials(b, h, 1)
                    if h + 2 < H or has_next:
                        stack_out(*((b, h + 2) if h + 2 < H else (nxt, h + 2 - H)))
                    if h + 3 < H or has_next:
                        stack_high(*((b, h + 3) if h + 3 < H else (nxt, h + 3 - H)))
                    if h + 1 < H or has_next:
                        row(*((b, h + 1) if h + 1 < H else (nxt, 0)))
                    if kind == 0 and (t > 0 or has_prev):
                        weighed_out(*group)
                    if kind == 0 and has_next:
                        move_out(b, TT + t, 2)
                    if kind == 0 and (t > 0 or has_prev):
                        copy_sums(*group)
                    if kind in (1, 2) and has_next:
                        move_out(b, TT + 1 + t, kind - 1)
                    if kind == 3 and has_next:
                        modulate(b, TT + 2 + t)

            b0, last = Batch(0), Batch(NB - 1)
            act.wait_ge(w_centred, 1)
            weight_high(0)
            act.wait_ge(ss_ready, 4)
            modulate(b0, 0)
            act.wait_ge(w_centred, 2)
            weight_high(1)
            act.wait_ge(ld_w[2], 16)
            weight_high(2)
            act.wait_ge(gate_product, 1)
            act.activation(gate_sb, M[0:NB, 1, :], ACT.Copy).then_inc(gate_ready, 1)
            for c in range(TT + 1):
                for j in range(3 if c < TT else 2):
                    move_out(b0, c, j)
                    if j == 0:
                        modulate(b0, c + 1)
            for h in range(2):
                stack_high(b0, h)
                stack_out(b0, h)
            stack_high(b0, 2)
            row(b0, 0)
            act.wait_ge(st_mod, 32)
            body(b0, True)
            with act.Fori(0, (NB - 2) // 2) as i:
                body(Batch(1, i), True)
                body(Batch(2, i), True)
            body(last, False)
            weighed_out(last, NG - 1)
            copy_sums(last, NG - 1)

        @block.vector
        def _(dve):
            dve.sem_inc(y_gated, 1)
            dve.wait_ge(consts, 6)
            dve.tensor_copy(ident_r[:], ident[:]).then_inc(ident_ready, 1)
            dve.wait_ge(cond_exp, 1)
            dve.tensor_scalar(silu_sb, silu_sb, 1.0, None, ALU.add).then_inc(silu_step, 1)
            dve.wait_ge(silu_step, 1)
            dve.reciprocal(silu_sb, silu_sb).then_inc(silu_step, 1)
            dve.wait_ge(silu_step, 2)
            dve.tensor_tensor(silu_sb, silu_sb, cond_sb, ALU.mult).then_inc(silu_ready, 1)
            dve.wait_ge(siluT_done, 1)
            dve.tensor_copy(modb_cols, TP[:, 0, DT * NB:DT * NB + 2 * DT]).then_inc(modb_ready, 1)
            dve.tensor_copy(siluT, TP[:, 0, 0:DT * NB].rearrange("p (c b) -> p c b", c=DT)
                            ).then_inc(siluT_ready, 1)
            dve.memset(stats[:], 1.0).then_inc(x_stats, 1)
            dve.wait_ge(x_stats, 1)

            NEWTON = 13

            def x_statistics(b, c):
                dve.wait_ge(ld_x[c % 2], b.at(16 * TT // 2, 16 * (c // 2 + 1)))
                if c > 0 or b.first > 0:
                    dve.wait_ge(x_stats, b.at(2 * TT, 2 * c + 1))
                dve.bn_stats(bn[:], xin[:, c % 2, :]).then_inc(x_stats, 1)

            def wait_to_aggregate(b, c):
                dve.wait_ge(x_stats, b.at(2 * TT, 2 * c + 2))
                if c > 0 or b.first > 0:
                    dve.wait_ge(x_norm, b.at(TT, c))

            def aggregate_x():
                dve.bn_aggr(stats[:, 0:2], bn[:]).then_inc(x_stats, 1)

            def square_sums(b, c, j):
                dve.wait_ge(squared, b.at(2 * TT, 2 * c + j + 1))
                dve.wait_ge(newton_step, b.at(NEWTON * TT, NEWTON * (c + 2)))
                dve.tensor_reduce(stats[:, 2 + j * H:2 + (j + 1) * H],
                                  squares[:].rearrange("p (h e) -> p h e", e=E), AX.X, ALU.add
                                  ).then_inc(ss_done, 1)

            def inverse_roots(b, c, first=1, last=NEWTON):
                if first == 1:
                    dve.wait_ge(x_stats, b.at(2 * TT, 2 * c + 3))
                    if c > 0 or b.first > 0:
                        dve.wait_ge(x_norm, b.at(TT, c))
                    if c > 1 or b.first > 0:
                        dve.wait_ge(ss_done, b.at(2 * TT, 2 * (c - 1)))
                    if c > 2 or b.first > 0:
                        dve.wait_ge(qk_norm, b.at(TT, c - 2))
                for n in range(first, last + 1):
                    if n > 1:
                        dve.wait_ge(newton_step, b.at(NEWTON * TT, NEWTON * c + n - 1))
                    if n == 1:
                        ins = dve.tensor_scalar(rstd[:], stats[:, 1:], EPS, None, ALU.add)
                    elif n == 2:
                        ins = dve.tensor_scalar(newton[:].bitcast(I32), rstd[:].bitcast(I32), 1, None,
                                                ALU.logical_shift_right)
                    elif n == 3:
                        ins = dve.tensor_scalar(half_var[:], rstd[:], -0.5, None, ALU.mult)
                    elif n == 4:
                        ins = dve.tensor_scalar(rstd[:].bitcast(I32), newton[:].bitcast(I32), -1.0,
                                                float(RSQRT_MAGIC), ALU.mult, ALU.add)
                    elif n % 3 == 2:
                        ins = dve.tensor_tensor(newton[:], rstd[:], rstd[:], ALU.mult)
                    elif n % 3 == 0:
                        ins = dve.tensor_tensor(newton[:], newton[:], half_var[:], ALU.mult)
                    else:
                        ins = dve.scalar_tensor_tensor(rstd[:], newton[:], 1.5, rstd[:], ALU.add, ALU.mult)
                    ins.then_inc(newton_step, 1)

            def normalize_x(b, c):
                dve.wait_ge(newton_step, b.at(NEWTON * TT, NEWTON * (c + 1)))
                xt = xin[:, c % 2, :]
                dve.tensor_scalar(xt, xt, stats[:, 0:1], rstd[:, 0:1], ALU.subtract, ALU.mult
                                  ).then_inc(x_norm, 1)

            def normalize_qk(b, c):
                dve.wait_ge(newton_step, b.at(NEWTON * TT, NEWTON * (c + 3)))
                dve.wait_ge(raw_out, b.at(2 * TT, 2 * c + 2))
                par = (b.first + c // TT) % 2
                qk = rows[:, par, c % TT, :, :].rearrange("p j (h e) -> p (j h) e", e=E)
                dve.tensor_tensor(qk, qk, rstd[:, 1:].unsqueeze(2).to_broadcast([P, 2 * H, E]), ALU.mult
                                  ).then_inc(qk_norm, 1)

            def x_parts(b, c):
                flat = "p c t -> p (c t)"
                dve.wait_ge(h_ready, b.at(TT, c + 1))
                x_hi, x_lo = x_buffers(b, c)
                if b.first > 0 or c > TT:
                    dve.wait_ge(proj_done, b.at(3 * TT, 3 * c))
                elif c > 1:
                    dve.wait_ge(proj_done, 3 * (c - 1))
                dve.tensor_copy(x_hi.rearrange(flat), hT[:].rearrange(flat)).then_inc(h_hi, 1)
                dve.wait_ge(h_hi, b.at(TT, c + 1))
                dve.tensor_tensor(x_lo.rearrange(flat), hT[:].rearrange(flat),
                                  x_hi.rearrange(flat).bitcast(F32), ALU.subtract).then_inc(h_lo, 1)

            def stack_low(b, h):
                dve.wait_ge(stack_hi, b.at(2 * H, 2 * h + 2))
                src = rows[:, b.parity, :, :, h * E:(h + 1) * E]
                dve.tensor_tensor(stack_at(2 * E, SK - E), src, stack_at(0, SK).bitcast(F32), ALU.subtract
                                  ).then_inc(stack_ready, 1)

            def maximum(b, h, t):
                dve.wait_ge(max_scores, b.at(TT * H, TT * h + t + 1))
                if t == 0 and (h > 1 or b.first > 0):
                    dve.wait_ge(row_done, b.at(H, h - 1))
                dve.tensor_reduce(neg_max[:, h % 2, t:t + 1], M[:, t % 2, :], AX.X, ALU.max, negate=True
                                  ).then_inc(max_out, 1)

            def invert_sums(b, g, n):
                if n == 0:
                    dve.wait_ge(sums_out, b.at(NG, g + 1))
                part = sums[:, n * P:(n + 1) * P]
                dve.reciprocal(part, part).then_inc(recip_done, 1)

            def normalize_o(b, g):
                dve.wait_ge(recip_done, b.at(TT * NG, TT * (g + 1)))
                dve.wait_ge(o_out, b.at(NG, g + 1))
                o = oT[:, b.parity, g, :]
                dve.tensor_tensor(o, o, sums[:], ALU.mult).then_inc(o_ready, 1)

            def apply_gate(b, t, bank):
                dve.wait_ge(y_done, b.at(TT, t + 1))
                if t == 0:
                    dve.wait_ge(ld_gate, b.at(16, 16))
                dve.wait_ge(y_ready, b.at(TT, t + 1))
                dve.tensor_tensor(gated[:], bank, gate[:], ALU.mult).then_inc(y_gated, 1)

            def body(b, has_next):
                has_prev = b.first > 0
                prev, nxt = b.plus(-1), b.plus(1)
                for h in range(H):
                    t, kind = h // 4, h % 4
                    c = TT + 1 + t
                    group = (b, t - 1) if t > 0 else (prev, NG - 1)
                    grouped = t > 0 or has_prev

                    def beside(place):
                        if kind == 0 and has_next and place == 1:
                            normalize_qk(b, c - 1)
                        if kind == 0 and has_next and place == 2:
                            x_parts(b, c)
                        if kind == 1 and grouped:
                            for n in range(TT):
                                if (1, 2, 3, 3)[n] == place:
                                    invert_sums(*group, n)
                        if kind == 2 and grouped and place == 1:
                            normalize_o(*group)
                        if kind == 2 and has_next and place == 2:
                            square_sums(b, c, 0)
                        if kind == 2 and has_next and place == 3:
                            x_statistics(b, c + 2)
                        if kind == 3 and has_next and place == 0:
                            wait_to_aggregate(b, c + 2)
                            square_sums(b, c, 1)
                            aggregate_x()
                            inverse_roots(b, c + 2, 1, 2)
                        if kind == 3 and has_next and place == 1:
                            inverse_roots(b, c + 2, 3, 6)
                        if kind == 3 and has_next and place == 2:
                            inverse_roots(b, c + 2, 7, NEWTON)
                        if kind == 3 and has_prev and place == 3:
                            apply_gate(prev, t, (O if has_next else Q)[:])
                        if kind == 3 and has_next and place == 3:
                            normalize_x(b, c + 2)

                    beside(0)
                    for n in range(TT):
                        if h + 1 < H or has_next:
                            maximum(*((b, h + 1) if h + 1 < H else (nxt, 0)), n)
                        if n == 1:
                            beside(1)
                    beside(2)
                    if h + 3 < H or has_next:
                        stack_low(*((b, h + 3) if h + 3 < H else (nxt, h + 3 - H)))
                    beside(3)

            b0, last = Batch(0), Batch(NB - 1)
            x_statistics(b0, 0)
            wait_to_aggregate(b0, 0)
            aggregate_x()
            inverse_roots(b0, 0)
            normalize_x(b0, 0)

            def weight_mean(j):
                dve.wait_ge(ld_w[j], 16)
                w = w_raw[:, :, j * D:(j + 1) * D].rearrange("p c (h e) -> p c h e", e=E)
                mean = w_mean[:, j]
                dve.tensor_reduce(mean, w, AX.X, ALU.add).then_inc(w_step, 1)
                dve.wait_ge(w_step, 2 * j + 1)
                dve.tensor_scalar(mean, mean, 1.0 / E, None, ALU.mult).then_inc(w_step, 1)

            def weight_centre(j):
                dve.wait_ge(w_step, 2 * j + 2)
                w = w_raw[:, :, j * D:(j + 1) * D].rearrange("p c (h e) -> p c h e", e=E)
                mean = w_mean[:, j]
                dve.tensor_tensor(w, w, mean.unsqueeze(3).to_broadcast([P, DT, H, E]), ALU.subtract
                                  ).then_inc(w_centred, 1)

            def weight_low(j):
                dve.wait_ge(w_high, j + 1)
                cols = slice(j * D, (j + 1) * D)
                dve.tensor_tensor(wqkv_lo[:, :, cols], w_raw[:, :, cols], wqkv_hi[:, :, cols].bitcast(F32),
                                  ALU.subtract).then_inc(w_low, 1)

            weight_mean(0)
            weight_centre(0)
            weight_mean(1)
            weight_low(0)
            dve.wait_ge(ss_product, 1)
            dve.wait_ge(modb_ready, 1)
            for m in range(2 * DT):
                ins = dve.tensor_scalar(ss_sb[:, :, m], M[:, 0, m * NB:(m + 1) * NB], modb_cols[:, m:m + 1],
                                        0.0 if m < DT else 1.0, ALU.add, ALU.add)
            ins.then_inc(ss_ready, 3)
            dve.wait_ge(ss_ready, 3)
            dve.tensor_copy(shift_scale[:], ss_sb[:, 0:2, :]).then_inc(ss_ready, 1)
            weight_centre(1)
            x_parts(b0, 0)
            x_statistics(b0, 1)
            wait_to_aggregate(b0, 1)
            aggregate_x()
            inverse_roots(b0, 1, 1, 4)
            weight_low(1)
            inverse_roots(b0, 1, 5, NEWTON)
            normalize_x(b0, 1)
            weight_low(2)
            dve.wait_ge(ld_tables, 16 * 3)
            for j in range(2):
                w = norm_w[:, j, 0:R].rearrange("p (i two) -> p i two", two=2)
                dve.tensor_copy(rope_same[:, :, j, R:E], norm_w[:, j, R:E].unsqueeze(1).to_broadcast([P, TT, R]))
                for t in range(TT):
                    pos = pos_sb[:, t, :].rearrange("p (i c) -> p i c", c=2)
                    dve.tensor_tensor(rope_same[:, t, j, 0:R].rearrange("p (i two) -> p i two", two=2),
                                      pos[:, :, 0:1].to_broadcast([P, PAIRS, 2]), w, ALU.mult)
                    dve.tensor_tensor(rope_pair[:, t, j, :].rearrange("p (i two) -> p i two", two=2),
                                      pos[:, :, 1:2].to_broadcast([P, PAIRS, 2]), w[:, :, ::-1], ALU.mult
                                      ).then_inc(table_step, 1)
            dve.wait_ge(table_step, 2 * TT)
            even = rope_pair[:].rearrange("p t j (i two) -> p (t j i) two", two=2)[:, :, 0:1]
            dve.tensor_scalar(even, even, -1.0, None, ALU.mult).then_inc(tables_ready, 1)
            for c in range(TT + 1):
                square_sums(b0, c, 0)
                x_statistics(b0, c + 2)
                if c < TT:
                    x_parts(b0, c + 1)
                wait_to_aggregate(b0, c + 2)
                square_sums(b0, c, 1)
                aggregate_x()
                inverse_roots(b0, c + 2)
                normalize_x(b0, c + 2)
                if c < TT:
                    normalize_qk(b0, c)
            stack_low(b0, 0)
            stack_low(b0, 1)
            for t in range(TT):
                maximum(b0, 0, t)
            stack_low(b0, 2)
            body(b0, True)
            with dve.Fori(0, (NB - 2) // 2) as i:
                body(Batch(1, i), True)
                body(Batch(2, i), True)
            body(last, False)
            for n in range(TT):
                invert_sums(last, NG - 1, n)
            normalize_o(last, NG - 1)
            dve.wait_ge(ld_last, 32)
            dve.wait_ge(ld_res[0], last.at(32, 16))
            dve.wait_ge(ld_res[1], last.at(32, 16))
            for t in range(TT):
                apply_gate(last, t, last_banks[t])
                dve.wait_ge(y_gated, last.at(TT, t + 2))
                dve.tensor_tensor(last_res[t], last_res[t], gated[:], ALU.add).then_inc(y_ready, 1)

        @block.gpsimd
        def _(pool):
            pool.sem_inc(y_ready, 1)
            pool.memset(ident[:], 0.0).then_inc(consts, 1)
            pool.wait_ge(consts, 1)
            pool.memset(ones[:], 1.0).then_inc(consts, 1)
            for n in range(2):
                pool.wait_ge(consts, 2 + n)
                pool.memset(stackT[SK:SK + 1, n, 1, :].bitcast(F32), 1.0).then_inc(consts, 1)
            pool.wait_ge(consts, 4)
            pool.affine_select(out=ident[:], in_=ident[:], compare_op=ALU.not_equal, fill=1.0, base=0,
                               pattern=[[-1, P]], channel_multiplier=1).then_inc(consts, 2)

            def rotate(b, c):
                pool.wait_ge(qk_norm, b.at(TT, c + 1))
                par, t = (b.first + c // TT) % 2, c % TT
                for j in range(2):
                    n = 6 * c + 3 * j
                    r = rows[:, par, t, j, :].rearrange("p (h e) -> p h e", e=E)
                    swapped = bass.AP(tensor=r.tensor, offset=r.offset + 1,
                                      ap=[r.ap[0], [E, H], [2, PAIRS], [-1, 2]])
                    if n > 0 or b.first > 0:
                        pool.wait_ge(rope_step, b.at(6 * TT, n))
                    pool.tensor_tensor(pair_part[:].rearrange("p h (i two) -> p h i two", two=2), swapped,
                                       rope_pair[:, t, j, :].rearrange("p (i two) -> p i two", two=2)
                                       .unsqueeze(1).to_broadcast([P, H, PAIRS, 2]), ALU.mult
                                       ).then_inc(rope_step, 1)
                    pool.wait_ge(rope_step, b.at(6 * TT, n + 1))
                    pool.tensor_tensor(r, r, rope_same[:, t, j, :].unsqueeze(1).to_broadcast([P, H, E]),
                                       ALU.mult).then_inc(rope_step, 1)
                    pool.wait_ge(rope_step, b.at(6 * TT, n + 2))
                    last = pool.tensor_tensor(r[:, :, 0:R], r[:, :, 0:R], pair_part[:], ALU.add)
                    last.then_inc(rope_step, 1)

            def sum_key_tiles(b, h):
                n = buf(h)
                before = h // HG - (2 if h % HG == 0 else 1)
                pool.wait_ge(exp_done, b.at(2 * H, 2 * h + 1))
                if before >= 0 or b.first > 0:
                    pool.wait_ge(sums_done, b.at(NG, before + 1))
                pool.tensor_tensor(colsum[:, n, :], probs[:, n, 0, :], probs[:, n, 1, :], ALU.add
                                   ).then_inc(sum_step, 1)
                pool.wait_ge(sum_step, b.at(2 * H, 2 * h + 1))
                pool.wait_ge(exp_done, b.at(2 * H, 2 * h + 2))
                pool.tensor_tensor(colsum[:, n, :], colsum[:, n, :], probs[:, n, 2, :], ALU.add
                                   ).then_inc(sum_step, 1)
                pool.wait_ge(sum_step, b.at(2 * H, 2 * h + 2))
                pool.tensor_tensor(colsum[:, n, :], colsum[:, n, :], probs[:, n, 3, :], ALU.add
                                   ).then_inc(sum_rows, 1)

            def add_residual(b, t):
                pool.wait_ge(y_gated, b.at(TT, t + 2))
                pool.wait_ge(ld_res[t % 2], b.at(32, 16 * (t // 2 + 1)))
                r = xres[:, t % 2, :]
                pool.tensor_tensor(r, r, gated[:], ALU.add).then_inc(y_ready, 1)

            def body(b, has_next):
                prev = b.plus(-1)
                for h in range(H):
                    t, kind = h // 4, h % 4
                    if kind == 0 and has_next:
                        rotate(b, TT + t)
                    sum_key_tiles(b, h)
                    if kind == 3 and b.first > 0:
                        add_residual(prev, t)

            b0, last = Batch(0), Batch(NB - 1)
            pool.wait_ge(tables_ready, 1)
            for t in range(TT):
                rotate(b0, t)
            body(b0, True)
            with pool.Fori(0, (NB - 2) // 2) as i:
                body(Batch(1, i), True)
                body(Batch(2, i), True)
            body(last, False)


_INS = ["x", "cond_1024", "L0_cond_position", "L0_cond_mod_w", "L0_cond_mod_b", "L0_cond_w_qkv",
        "L0_cond_w_out", "L0_cond_q_norm_w", "L0_cond_k_norm_w"]


def kernel(**inputs):
    import numpy as _np
    import concourse.bacc as _bacc
    from concourse import mybir as _mybir
    from concourse.bass_utils import run_bass_kernel_spmd as _run

    nc = _bacc.Bacc("TRN2", target_bir_lowering=False, num_devices=1)
    arrays, args = {}, []
    for name in _INS:
        a = _np.ascontiguousarray(inputs[name])
        arrays[f"in_{name}_dram"] = a
        args.append(nc.dram_tensor(f"in_{name}_dram", a.shape, _mybir.dt.from_np(a.dtype),
                                   kind="ExternalInput").ap())
    shape = tuple(inputs["x"].shape)
    args.append(nc.dram_tensor("out_0_dram", shape, _mybir.dt.float32, kind="ExternalOutput").ap())
    cond_attention_kernel(nc, *args)
    r = _run(nc, [arrays], core_ids=[0])
    return r.results[0]["out_0_dram"]
```
